# Optimizing a Trainium2 kernel written in Bass

```python
import numpy as np
import jax
import jax.numpy as jnp

def _softmax(x, axis=-1):
    return jax.nn.softmax(x, axis=axis)

def _gelu(x):
    return jax.nn.gelu(x, approximate=True)

def _silu(x):
    return jax.nn.silu(x)

def _sigmoid(x):
    return jax.nn.sigmoid(x)

def _layernorm(x, axis=-1, eps=1e-05):
    m = jnp.mean(x, axis=axis, keepdims=True)
    v = jnp.var(x, axis=axis, keepdims=True)
    return (x - m) / jnp.sqrt(v + eps)

def _scatter_add(tgt, idx, src, axis=0):
    return tgt.at[idx].add(src)

def _segment_sum(src, seg, n):
    return jax.ops.segment_sum(src, seg, n)
kernel_name = 'mk_adaln_ffn_d1_seqx_r2_74cfd7'

def setup_inputs(seed: int=0):
    np.random.seed(seed)
    _w = jnp.asarray

    def _rec_inputs():
        import jax
        import jax.numpy as jnp
        _rk = jax.random.key(seed)
        x = 7.971e-05 + 1 * jax.random.normal(jax.random.fold_in(_rk, 1), (16, 512, 512), jnp.float32)
        _lenS = 512 - jax.random.randint(jax.random.fold_in(_rk, 7), (16,), 0, max(1, 512 // 4) + 1, jnp.int32)
        _lenS2 = 512 - jax.random.randint(jax.random.fold_in(_rk, 8), (16,), 0, max(1, 512 // 4) + 1, jnp.int32)
        itok_B_0_6 = jax.random.randint(jax.random.fold_in(_rk, 11), (16,), 0, 7, jnp.int32)
        return (x, itok_B_0_6)
    x, itok_B_0_6 = _rec_inputs()

    def _L0_cond_setup():
        import jax, jax.numpy as jnp
        import numpy as np
        N_PROFILES = 8
        HIDDEN = 512
        BOTTLENECK = 128
        EPS = 1e-05
        key = jax.random.key(seed)
        ks = jax.random.split(key, 8)
        B, S, H, K, P = (16, 1024, HIDDEN, BOTTLENECK, N_PROFILES)
        down_w = jax.random.normal(ks[0], (P, H, K), dtype=jnp.float32) * (1.0 / np.sqrt(H))
        down_b = jax.random.normal(ks[1], (P, K), dtype=jnp.float32) * 0.01
        up_w = jax.random.normal(ks[2], (P, K, H), dtype=jnp.float32) * (1.0 / np.sqrt(K))
        up_b = jax.random.normal(ks[3], (P, H), dtype=jnp.float32) * 0.01
        ln_g = jnp.ones((P, H), dtype=jnp.float32)
        ln_b = jnp.zeros((P, H), dtype=jnp.float32)
        hidden = jax.random.normal(ks[4], (B, S, H), dtype=jnp.float32)
        profile_ids = jax.random.randint(ks[5], (B,), 0, P)
        return {'hidden': hidden, 'profile_ids': profile_ids, 'down_w': down_w, 'down_b': down_b, 'up_w': up_w, 'up_b': up_b, 'ln_g': ln_g, 'ln_b': ln_b}
    _L0_cond_all = _L0_cond_setup()
    _L0_cond_in = {k: v for k, v in _L0_cond_all.items() if k in ('down_w', 'down_b', 'up_w', 'up_b', 'ln_g', 'ln_b')}
    del _L0_cond_all

    def _L0_ffn_setup():
        import jax, jax.numpy as jnp
        import numpy as np
        BLOCK = 32
        W_BITS = 4
        ACT_BITS = 16

        def act_qdq(x):
            qmax = 2.0 ** (ACT_BITS - 1) - 1.0
            scale = jnp.maximum(jnp.max(jnp.abs(x)) / qmax, 1e-12)
            return jnp.clip(jnp.round(x / scale), -qmax - 1.0, qmax) * scale

        def fixed_qdq_u16(x):
            scale = 1.0 / 65536.0
            return jnp.clip(jnp.round(x / scale), 0.0, 65535.0) * scale

        def lpbq_dequant(w):
            O, I = w.shape
            qmax = 2.0 ** (W_BITS - 1) - 1.0
            wb = w.reshape(O, I // BLOCK, BLOCK)
            s = jnp.maximum(jnp.max(jnp.abs(wb), axis=-1, keepdims=True) / qmax, 1e-12)
            wq = jnp.clip(jnp.round(wb / s), -qmax - 1.0, qmax) * s
            return wq.reshape(O, I)
        key = jax.random.key(seed)
        k1, k2, k3, k4 = jax.random.split(key, 4)
        B, S, H, I = (2, 2048, 512, 1536)
        x = jax.random.normal(k1, (B, S, H), jnp.float32)
        w_gate = jax.random.normal(k2, (I, H), jnp.float32) * 0.02
        w_up = jax.random.normal(k3, (I, H), jnp.float32) * 0.02
        w_down = jax.random.normal(k4, (H, I), jnp.float32) * 0.02
        return {'x': x, 'w_gate': w_gate, 'w_up': w_up, 'w_down': w_down}
    _L0_ffn_all = _L0_ffn_setup()
    _L0_ffn_in = {k: v for k, v in _L0_ffn_all.items() if k in ('w_gate', 'w_up', 'w_down')}
    del _L0_ffn_all
    return {'x': x, 'itok_B_0_6': itok_B_0_6, 'L0_cond_down_w': _L0_cond_in['down_w'], 'L0_cond_down_b': _L0_cond_in['down_b'], 'L0_cond_up_w': _L0_cond_in['up_w'], 'L0_cond_up_b': _L0_cond_in['up_b'], 'L0_cond_ln_g': _L0_cond_in['ln_g'], 'L0_cond_ln_b': _L0_cond_in['ln_b'], 'L0_ffn_w_gate': _L0_ffn_in['w_gate'], 'L0_ffn_w_up': _L0_ffn_in['w_up'], 'L0_ffn_w_down': _L0_ffn_in['w_down']}

def reference(x, itok_B_0_6, L0_cond_down_w, L0_cond_down_b, L0_cond_up_w, L0_cond_up_b, L0_cond_ln_g, L0_cond_ln_b, L0_ffn_w_gate, L0_ffn_w_up, L0_ffn_w_down):
    import jax
    import jax.numpy as jnp

    def _L0_cond_ref(hidden, profile_ids, down_w, down_b, up_w, up_b, ln_g, ln_b):
        import jax, jax.numpy as jnp
        import numpy as np
        N_PROFILES = 8
        HIDDEN = 512
        BOTTLENECK = 128
        EPS = 1e-05
        Wd = down_w[profile_ids]
        bd = down_b[profile_ids][:, None]
        Wu = up_w[profile_ids]
        bu = up_b[profile_ids][:, None]
        g = ln_g[profile_ids][:, None]
        b = ln_b[profile_ids][:, None]
        z = jax.nn.relu(jnp.einsum('bsh,bhk->bsk', hidden, Wd) + bd)
        y = hidden + jnp.einsum('bsk,bkh->bsh', z, Wu) + bu
        mu = jnp.mean(y, axis=-1, keepdims=True)
        var = jnp.mean(jnp.square(y - mu), axis=-1, keepdims=True)
        return (y - mu) * jax.lax.rsqrt(var + EPS) * g + b

    def _L0_ffn_ref(x, w_gate, w_up, w_down):
        import jax, jax.numpy as jnp
        import numpy as np
        BLOCK = 32
        W_BITS = 4
        ACT_BITS = 16

        def act_qdq(x):
            qmax = 2.0 ** (ACT_BITS - 1) - 1.0
            scale = jnp.maximum(jnp.max(jnp.abs(x)) / qmax, 1e-12)
            return jnp.clip(jnp.round(x / scale), -qmax - 1.0, qmax) * scale

        def fixed_qdq_u16(x):
            scale = 1.0 / 65536.0
            return jnp.clip(jnp.round(x / scale), 0.0, 65535.0) * scale

        def lpbq_dequant(w):
            O, I = w.shape
            qmax = 2.0 ** (W_BITS - 1) - 1.0
            wb = w.reshape(O, I // BLOCK, BLOCK)
            s = jnp.maximum(jnp.max(jnp.abs(wb), axis=-1, keepdims=True) / qmax, 1e-12)
            wq = jnp.clip(jnp.round(wb / s), -qmax - 1.0, qmax) * s
            return wq.reshape(O, I)
        x = act_qdq(x)
        up = act_qdq(x @ lpbq_dequant(w_up).T)
        gate = act_qdq(x @ lpbq_dequant(w_gate).T)
        sig = fixed_qdq_u16(jax.nn.sigmoid(gate))
        gate = act_qdq(gate * sig)
        o = act_qdq(gate * up)
        return o @ lpbq_dequant(w_down).T
    x = x + _L0_ffn_ref(_L0_cond_ref(x, itok_B_0_6, L0_cond_down_w, L0_cond_down_b, L0_cond_up_w, L0_cond_up_b, L0_cond_ln_g, L0_cond_ln_b), L0_ffn_w_gate, L0_ffn_w_up, L0_ffn_w_down)
    return x

_drawn_inputs = setup_inputs


def setup_inputs(seed=0):
    import zlib

    import numpy as np

    out = dict(_drawn_inputs(seed))
    spreads = {'L0_cond_ln_g': (1.0, 0.542), 'L0_cond_ln_b': (0.0, 0.574)}
    factors = {'L0_cond_down_b': 33.127, 'L0_cond_up_b': 25.468}
    for name, (base, spread) in spreads.items():
        noise = np.random.default_rng([zlib.crc32(name.encode()), seed]).standard_normal(out[name].shape)
        drawn = base * np.exp(spread * noise) if base else spread * noise
        out[name] = jnp.asarray(drawn.astype(out[name].dtype))
    for name, factor in factors.items():
        out[name] = (out[name] * factor).astype(out[name].dtype)
    return out
```

```python
import concourse.bass as bass
from concourse import mybir
from contextlib import ExitStack

F32, F16, BF16 = mybir.dt.float32, mybir.dt.float16, mybir.dt.bfloat16
I16, U16, I32, U32 = mybir.dt.int16, mybir.dt.uint16, mybir.dt.int32, mybir.dt.uint32
ALU = mybir.AluOpType
ACT = mybir.ActivationFunctionType
AX = mybir.AxisListType

P = 128
B, S, H = 16, 512, 512
KB = 128
I = 1536
HK = H // P
ST = S // P
TILE = HK * S
NB = 4
CH = NB * S
CPB = I // P // NB
NCH = B * CPB
SL = 1536
NSL = 4
BLK = 32
NS = I * H // BLK // P
LN_EPS = 1e-5
QA = 32767.0
QW = 7.0
TINY = 1e-12
SIGQ = 65536.0
W_TOP = 4096.0
NEG_BOUND = 0.28
PARTS = 3
MARGIN = -36000.0


def adaln_ffn(nc, x, xT, ids, wd_dn, wu_dn, upb, cols, wnat, wtr, out):
    h_scr = nc.dram_tensor("h_scr", (B, P, TILE), F32).ap()
    s_scr = nc.dram_tensor("s_scr", (3, P, NS), F32).ap()
    r_scr = nc.dram_tensor("r_scr", (3, P, NS), F32).ap()
    gate_scr = nc.dram_tensor("gate_scr", (NCH, P, CH), F32).ap()
    up_scr = nc.dram_tensor("up_scr", (NCH, P, CH), F32).ap()
    b_scr = nc.dram_tensor("b_scr", (upb.shape[0], PARTS, H), BF16).ap()
    g_scr = nc.dram_tensor("g_scr", (NCH, P, CH), I16).ap()

    with ExitStack() as ctx:
        def sb(name, shape, dt):
            return ctx.enter_context(nc.sbuf_tensor(name, shape, dt))

        def sem(name):
            return ctx.enter_context(nc.semaphore(name))

        def pair(name):
            return [sem(name + "0"), sem(name + "1")]

        w_hi = sb("w_hi", [P, 3 * NSL, SL], F16)
        w_lo = sb("w_lo", [P, 3 * NSL, SL], F16)
        hq_mem = sb("hq_mem", [P, B * TILE // 2], F32)
        arena = sb("arena", [P, 15872], F32)
        ident = sb("ident", [P, P], F32)
        ones = sb("ones", [PARTS, P], BF16)
        n_prof = upb.shape[0]
        bias_rest = sb("bias_rest", [n_prof, H], F32)
        bias_part = sb("bias_part", [n_prof, PARTS, H], BF16)
        ids_sb = sb("ids_sb", [1, B], I32)
        flag_sb = sb("flag_sb", [P, 1], I32)
        hmax = sb("hmax", [P, B], F32)
        gmax = sb("gmax", [P, 2, NCH], F32)
        umax = sb("umax", [P, NCH], F32)
        rmax = sb("rmax", [P, NCH + 1], F32)
        rall = sb("rall", [P, NCH + 1], F32)
        top = sb("top", [P, 8], F32)
        top_at = sb("top_at", [P, 8], U32)
        flag2_sb = sb("flag2_sb", [P, 1], I32)
        omax = sb("omax", [P, NCH + 1], F32)
        fmax = sb("fmax", [P, NCH], F32)
        K = sb("K", [P, 64], F32)
        gu_max = sb("gu_max", [P, 1], F32)

        def carve(mem, at, cols_, dt):
            size = 2 if dt in (F16, I16, U16, BF16) else 4
            v = mem[:, at // 4:(at + cols_ * size) // 4]
            return v if dt == F32 else v.bitcast(dt)

        hq = hq_mem[:, :].bitcast(I16)

        pw, pr, ps_ = [carve(arena, a, SL, F32) for a in (0, 6144, 12288)]
        pq = carve(arena, 18432, SL, I16)
        def mem3(mem, at, a, b):
            return carve(mem, at, a * b, F32).rearrange("p (a b) -> p a b", a=a)
        wm1 = w_hi[:, NSL:, :].rearrange("p a b -> p (a b)").bitcast(F32)
        wm2 = w_lo[:, NSL:, :].rearrange("p a b -> p (a b)").bitcast(F32)
        R4 = range(4)
        nat = [[carve(arena, 21504 + p * 8192, 2048, F32) for p in range(2)],
               [carve(wm1, p * 8192, 2048, F32) for p in range(2)]]

        def small(mem, at, m):
            return [carve(mem, at + k * m * NS * 4, m * NS, F32) for k in range(5)]
        nat_m, nat_s, nat_t, nat_r, nat_c = zip(small(arena, 37888, 1), small(wm2, 0, 2))
        xin = [mem3(hq_mem, p * 8192, ST, H) for p in R4]
        xtin = [mem3(hq_mem, 32768 + p * 8192, HK, S) for p in R4]
        wdn = [mem3(wm1, p * 2048, HK, KB) for p in R4]
        wup = [carve(wm1, 8192 + p * 2048, H, F32) for p in R4]
        bup = [wm1[0:PARTS, (16384 + p * 1024) // 4:(17408 + p * 1024) // 4].bitcast(BF16) for p in R4]
        zsb = [carve(wm2, p * 2048, S, F32) for p in range(2)]
        hT = [mem3(wm2, 4096 + p * 8192, HK, S) for p in range(2)]
        col = [carve(wm2, 20480 + p * 64, 9, F32) for p in R4]
        bst = [mem3(wm2, 20736 + p * 128, ST, 6) for p in range(2)]
        mu, mv, ve, sd, rs, n1, n2, rr = [[carve(wm2, 20992 + n * 32 + p * 16, ST, F32) for p in range(2)]
                                          for n in range(8)]

        hin = carve(arena, 21504, TILE, F32)
        a_hi = [carve(arena, 29696 + p * 4096, TILE, F16) for p in range(2)]
        a_lo = [carve(arena, 37888 + p * 4096, TILE, F16) for p in range(2)]
        raw = [carve(arena, 46080 + p * 8192, CH, F32) for p in range(2)]
        assert 46080 + 16384 <= 15872 * 4
        gin = [carve(arena, p * 8192, CH, F32) for p in range(2)]
        wg1 = w_hi[:, 0:NSL, :].rearrange("p a b -> p (a b)").bitcast(F32)
        wg2 = w_lo[:, 0:NSL, :].rearrange("p a b -> p (a b)").bitcast(F32)
        su16 = carve(arena, 20480, CH, U16)
        gg = [carve(arena, 24576, CH, I16), carve(wg1, 8192, CH, I16)]
        up_abs = carve(wg1, 0, CH, F32)
        sig = carve(wg2, 0, CH, F32)
        gq = carve(wg2, 8192, CH, I16)

        gin2 = [carve(arena, p * 4096, CH, I16) for p in range(2)]
        pin2 = [carve(arena, 8192 + p * 8192, CH, F32) for p in range(2)]
        uq = [carve(arena, 24576 + p * 4096, CH, I16) for p in range(2)]
        g_top, u_top = [carve(hq_mem, 49152 + p * 4096, CH, I16) for p in range(2)]
        p_top = carve(hq_mem, 57344, CH, F32)
        prod = carve(arena, 32768, CH, F32)
        oq = carve(arena, 40960, CH, I16)
        o_hi = [carve(hq_mem, p * 4096, CH, F16) for p in range(2)]
        o_lo = [carve(hq_mem, 8192 + p * 4096, CH, F16) for p in range(2)]
        xres = [mem3(hq_mem, 16384 + p * 8192, ST, H) for p in range(2)]
        osb = [mem3(hq_mem, 32768 + p * 8192, ST, H) for p in range(2)]

        psum = ctx.enter_context(nc.psum_tensor("psum", [P, 8, 512], F32))
        half = [psum[:, 4 * p:4 * p + 4, :] for p in range(2)]
        half1 = [h.rearrange("p a n -> p (a n)") for h in half]
        pz, py, ptr = [0, 1], [2, 3], 4

        names = ("smax0 smax1 smax2 sall0 sall1 sall2 F0 F1 F2 Fi0 Fi1 Fi2 hm hma sh rh "
                 "gm gp gma gpa shg sg rg cq qf fsig fu fpos fm fma fsel sf rf cG sgn um uma shu su ru cu "
                 "om oma sfu so ro cO cD gap nb near").split()

        def k(n, w=1):
            a = names.index(n)
            return K[:, a:a + w]

        ids_in = sem("ids_in")
        const_ok = sem("const_ok")
        kstep = sem("kstep")
        nat_in, nat_red = pair("nat_in"), sem("nat_red")
        bias_in, bias_step, bias_ok, bias_out = sem("bias_in"), sem("bias_step"), sem("bias_ok"), sem("bias_out")
        smax_ok, sall_ok = sem("smax_ok"), sem("sall_ok")
        scales_ok, scr_out = sem("scales_ok"), sem("scr_out")
        prep_in, prep_q = sem("prep_in"), sem("prep_q")
        prep_w, prep_hi, prep_lo = sem("prep_w"), sem("prep_hi"), sem("prep_lo")
        in_a = [sem("in_a%d" % p) for p in range(4)]
        z_done, z_act, y_done, y_added = sem("z_done"), sem("z_act"), sem("y_done"), sem("y_added")
        bn_done, ag_done, var_ok, std_ok = sem("bn_done"), sem("ag_done"), sem("var_ok"), sem("std_ok")
        newton, yn_ok, tr_done, h_evac = sem("newton"), sem("yn_ok"), sem("tr_done"), sem("h_evac")
        hmax_ok, h_stored = sem("hmax_ok"), pair("h_stored")
        hm_ok, hma_ok = sem("hm_ok"), sem("hma_ok")
        hin_in, hq_ok, hi_ok, split_ok = sem("hin_in"), sem("hq_ok"), sem("hi_ok"), sem("split_ok")
        g_mm, g_evac, g_red, g_stored = sem("g_mm"), pair("g_evac"), pair("g_red"), pair("g_stored")
        gm_ok, gma_ok, fsig_ok, flag_ok = sem("gm_ok"), sem("gma_ok"), sem("fsig_ok"), sem("flag_ok")
        f_in, f_q, f_sig, f_u, f_f = pair("f_in"), sem("f_q"), sem("f_sig"), sem("f_u"), sem("f_f")
        f_red, f_max, f_all, cg_ok = sem("f_red"), sem("f_max"), sem("f_all"), sem("cg_ok")
        hi2_ok, split2_ok = sem("hi2_ok"), sem("split2_ok")
        u_mm, u_evac, u_red, u_stored = sem("u_mm"), pair("u_evac"), pair("u_red"), pair("u_stored")
        gin_in, gq_ok, sig_ok, su_ok = pair("gin_in"), sem("gq_ok"), sem("sig_ok"), sem("su_ok")
        gg_ok, gg_stored = sem("gg_ok"), pair("gg_stored")
        um_ok, uma_ok, top_ok, cu_ok, flag2_ok = sem("um_ok"), sem("uma_ok"), sem("top_ok"), sem("cu_ok"), sem("flag2_ok")
        up_abs_ok, u_rmax = sem("up_abs_ok"), sem("u_rmax")
        d_in, d_uq, d_prod, d_red = sem("d_in"), sem("d_uq"), sem("d_prod"), sem("d_red")
        om_ok, oma_ok = sem("om_ok"), sem("oma_ok")
        e_in, e_uq, e_oq, e_hi, e_split = pair("e_in"), sem("e_uq"), sem("e_oq"), sem("e_hi"), sem("e_split")
        e_mm, x_in, res_ok, o_stored = sem("e_mm"), pair("x_in"), pair("res_ok"), pair("o_stored")

        def wait(engine, semaphore, value):
            if not (isinstance(value, int) and value <= 0):
                engine.wait_ge(semaphore, value)

        block = ctx.enter_context(nc.Block())

        @block.sync
        def _(sp):
            sp.dma_start(ids_sb[:, :], ids).then_inc(ids_in, 16)
            sp.dma_start(bias_rest[:, :], upb).then_inc(bias_in, 16)

            def load_blocks(group, m, n0):
                for part in range(3):
                    n = n0 + part
                    wait(sp, nat_red, n - 1 if n not in (3, 4) else 0)
                    sp.dma_start(nat[group][n % 2], wnat[m, :, part * 2048:(part + 1) * 2048]).then_inc(nat_in[n % 2], 16)

            s_rows = s_scr.rearrange("m p n -> (m p n)").rearrange("(s q c) -> s q c", q=4, c=SL)
            r_rows = r_scr.rearrange("m p n -> (m p n)").rearrange("(s q c) -> s q c", q=4, c=SL)

            def spill_scales(group, ms, done):
                sp.wait_ge(scales_ok, group + 1)
                for n, m in enumerate(ms):
                    for scr, src in ((s_scr, nat_c), (r_scr, nat_r)):
                        sp.dma_start(scr[m], src[group][:, n * NS:(n + 1) * NS]).then_inc(scr_out, 16)
                sp.wait_ge(scr_out, done)

            def load_slice(s):
                sp.dma_start(pw, wtr[bass.ds(s, 1)].rearrange("a p n -> p (a n)")).then_inc(prep_in, 16)
                for q in range(4):
                    for dst, rows in ((ps_, s_rows), (pr, r_rows)):
                        src = rows[bass.ds(s, 1), q, :].partition_broadcast(BLK)
                        sp.dma_start(dst[32 * q:32 * q + 32, :], src.rearrange("r a n -> r (a n)")).then_inc(prep_in, 16)

            sp.wait_ge(ids_in, 16)

            def load_batch(b, s, first=False):
                p = sp.value_load(ids_sb[0:1, bass.ds(b, 1)], min_val=0, max_val=n_prof - 1)
                sp.dma_start(xtin[s], xT[bass.ds(b, 1)].rearrange("a (k p) t -> p (a k) t", p=P)).then_inc(in_a[s], 16)
                sp.dma_start(wdn[s], wd_dn[bass.ds(p, 1)].rearrange("a (k p) n -> p (a k) n", p=P)).then_inc(in_a[s], 16)
                sp.dma_start(col[s], cols[bass.ds(p, 1)].rearrange("a p n -> p (a n)")).then_inc(in_a[s], 16)
                sp.dma_start(wup[s], wu_dn[bass.ds(p, 1)].rearrange("a p n -> p (a n)")).then_inc(in_a[s], 16)
                if first:
                    sp.wait_ge(bias_ok, 1)
                    sp.dma_start(b_scr, bias_part[:, :, :]).then_inc(bias_out, 16)
                    sp.wait_ge(bias_out, 16)
                sp.dma_start(bup[s], b_scr[bass.ds(p, 1)].rearrange("a r n -> (a r) n")).then_inc(in_a[s], 16)
                sp.dma_start(xin[s], x[bass.ds(b, 1)].rearrange("a (t p) h -> p (a t) h", p=P)).then_inc(in_a[s], 16)

            def store_h(b, s):
                sp.wait_ge(h_evac, 4 * b + 4)
                sp.dma_start(h_scr[bass.ds(b, 1)].rearrange("a p n -> p (a n)"),
                             hT[s].rearrange("p k n -> p (k n)")).then_inc(h_stored[s], 16)

            load_batch(0, 0, True)
            load_batch(1, 1)
            load_batch(2, 2)
            load_blocks(0, 0, 0)
            load_batch(3, 3)
            spill_scales(0, [0], 32)
            load_slice(0)
            with sp.Fori(0, B // 4 - 1) as i:
                for r in R4:
                    store_h(4 * i + r, r % 2)
                    load_batch(4 * i + r + 4, r)
                sp.wait_ge(prep_lo, i + 1)
                load_slice(i + 1)
            for b in range(B - 4, B):
                store_h(b, b % 2)

            sp.wait_ge(h_stored[0], 16 * B // 2)
            sp.wait_ge(h_stored[1], 16 * B // 2)

            def load_h(j):
                sp.dma_start(hin, h_scr[bass.ds(j, 1)].rearrange("a p n -> p (a n)")).then_inc(hin_in, 16)

            def store_raw(n, m, evac, scr, stored, uses):
                sp.wait_ge(evac[m % 2], uses + 1)
                sp.dma_start(scr[bass.ds(n, 1)].rearrange("a p n -> p (a n)"), raw[m % 2]).then_inc(stored[m % 2], 16)

            load_h(0)
            sp.wait_ge(hq_ok, 1)
            load_h(1)
            load_blocks(1, 1, 3)
            load_blocks(1, 2, 6)
            spill_scales(1, [1, 2], 96)
            load_slice(NSL)
            with sp.Fori(0, B // 2 - 1) as i:
                for u in range(2):
                    for c in range(CPB):
                        m = CPB * u + c
                        store_raw(6 * i + m, m, g_evac, gate_scr, g_stored, 3 * i + m // 2)
                    sp.wait_ge(hq_ok, 2 * i + u + 2)
                    load_h(2 * i + u + 2)
                sp.wait_ge(prep_lo, NSL + 1 + i)
                load_slice(NSL + 1 + i)
            for m in range(6):
                store_raw(42 + m, m, g_evac, gate_scr, g_stored, 21 + m // 2)
            sp.wait_ge(g_stored[0], 16 * NCH // 2)
            sp.wait_ge(g_stored[1], 16 * NCH // 2)
            sp.wait_ge(prep_lo, 3 * NSL)

            def load_gate(n, p, done):
                sp.dma_start(gin[p], gate_scr[bass.ds(n, 1)].rearrange("a p n -> p (a n)")).then_inc(done[p], 16)

            sp.wait_ge(flag_ok, 1)
            flag = sp.value_load(flag_sb[0:1, 0:1], min_val=0, max_val=1)
            with sp.If(flag > 0):
                load_gate(0, 0, f_in)
                load_gate(1, 1, f_in)
                with sp.Fori(1, NCH // 2) as i:
                    for p in range(2):
                        sp.wait_ge(f_q, 2 * i + p - 1)
                        load_gate(2 * i + p, p, f_in)
                sp.wait_ge(f_q, NCH)
            load_gate(0, 0, gin_in)
            load_gate(1, 1, gin_in)

            def up_chunk(n, m, uses, last):
                store_raw(n, m, u_evac, up_scr, u_stored, uses)
                sp.wait_ge(gg_ok, n + 1)
                if not last:
                    load_gate(n + 2, m % 2, gin_in)
                sp.dma_start(g_scr[bass.ds(n, 1)].rearrange("a p n -> p (a n)"), gg[m % 2]).then_inc(gg_stored[m % 2], 16)

            with sp.Fori(0, B // 2 - 1) as i:
                for m in range(6):
                    up_chunk(6 * i + m, m, 3 * i + m // 2, False)
            for m in range(6):
                up_chunk(42 + m, m, 21 + m // 2, m >= 4)
            for p in range(2):
                sp.wait_ge(u_stored[p], 16 * NCH // 2)
                sp.wait_ge(gg_stored[p], 16 * NCH // 2)

            def load_top(n):
                sp.dma_start(p_top, up_scr[bass.ds(n, 1)].rearrange("a p n -> p (a n)")).then_inc(d_in, 16)
                sp.dma_start(g_top, g_scr[bass.ds(n, 1)].rearrange("a p n -> p (a n)")).then_inc(d_in, 16)

            def load_gu(n, p, done):
                sp.dma_start(gin2[p], g_scr[bass.ds(n, 1)].rearrange("a p n -> p (a n)")).then_inc(done[p], 16)
                sp.dma_start(pin2[p], up_scr[bass.ds(n, 1)].rearrange("a p n -> p (a n)")).then_inc(done[p], 16)

            sp.wait_ge(top_ok, 1)
            load_top(sp.value_load(top_at[0:1, 0:1], min_val=0, max_val=NCH - 1))
            load_gu(0, 0, e_in)
            load_gu(1, 1, e_in)
            sp.wait_ge(flag2_ok, 1)
            flag2 = sp.value_load(flag2_sb[0:1, 0:1], min_val=0, max_val=1)
            with sp.If(flag2 > 0):
                with sp.Fori(0, NCH) as i:
                    sp.wait_ge(d_prod, i + 1)
                    load_top(i)

            def load_x(j, s):
                sp.dma_start(xres[s], x[bass.ds(j, 1)].rearrange("a (t p) h -> p (a t) h", p=P)).then_inc(x_in[s], 16)

            load_x(0, 0)
            load_x(1, 1)
            with sp.Fori(0, B // 2 - 1) as i:
                for m in range(6):
                    sp.wait_ge(e_oq, 6 * i + m + 1)
                    load_gu(6 * i + m + 2, m % 2, e_in)
                    if m == 4:
                        sp.wait_ge(res_ok[0], i + 1)
                        load_x(2 * i + 2, 0)
                sp.wait_ge(res_ok[1], i + 1)
                load_x(2 * i + 3, 1)
            for m in range(4):
                sp.wait_ge(e_oq, 42 + m + 1)
                load_gu(42 + m + 2, m % 2, e_in)
            sp.wait_ge(o_stored[0], 16 * B // 2)
            sp.wait_ge(o_stored[1], 16 * B // 2)

        @block.gpsimd
        def _(pool):
            RMAX = bass.bass_isa.ReduceOp.max
            nc.gpsimd.memset(ident[:, :], 0.0).then_inc(const_ok, 1)
            nc.gpsimd.memset(ones[:, :], 1.0).then_inc(const_ok, 1)
            pool.wait_ge(const_ok, 2)
            nc.gpsimd.affine_select(out=ident[:, :], in_=ident[:, :], compare_op=ALU.not_equal, fill=1.0,
                                    base=0, pattern=[[-1, P]], channel_multiplier=1).then_inc(const_ok, 1)

            def all_max(after, count, src, dst, done):
                pool.wait_ge(after, count)
                nc.gpsimd.partition_all_reduce(dst, src, P, RMAX).then_inc(done, 1)

            def w_lower(s):
                pool.wait_ge(prep_hi, s + 1)
                nc.gpsimd.tensor_tensor(w_lo[:, bass.ds(s, 1), :].rearrange("p a n -> p (a n)"), pw,
                                        w_hi[:, bass.ds(s, 1), :].rearrange("p a n -> p (a n)"),
                                        ALU.subtract).then_inc(prep_lo, 1)

            all_max(smax_ok, 1, k("smax0"), k("sall0"), sall_ok)
            with pool.Fori(0, NSL) as i:
                w_lower(i)
            all_max(hm_ok, 1, k("hm"), k("hma"), hma_ok)
            all_max(smax_ok, 2, k("smax1", 2), k("sall1", 2), sall_ok)
            with pool.Fori(0, 2 * NSL) as i:
                w_lower(NSL + i)
            all_max(gm_ok, 1, k("gm", 2), k("gma", 2), gma_ok)
            pool.wait_ge(flag_ok, 1)
            flag = pool.value_load(flag_sb[0:1, 0:1], min_val=0, max_val=1)
            with pool.If(flag > 0):
                all_max(f_max, 1, k("fm"), k("fma"), f_all)
            all_max(um_ok, 1, rmax[:, :], rall[:, :], uma_ok)
            all_max(om_ok, 1, k("om"), k("oma"), oma_ok)

        @block.scalar
        def _(act):
            def w_upper(s):
                act.wait_ge(prep_w, s + 1)
                nc.scalar.activation(w_hi[:, bass.ds(s, 1), :].rearrange("p a n -> p (a n)"), pw,
                                     ACT.Copy).then_inc(prep_hi, 1)

            def relu(i, o):
                b, r = 4 * i + o, o % 4
                act.wait_ge(z_done, b + 1)
                if not (isinstance(b, int) and b < 2):
                    act.wait_ge(y_done, 4 * b - 4)
                nc.scalar.activation(zsb[r % 2], psum[:, pz[r % 2], :], ACT.Relu, bias=col[r][:, 8:9]).then_inc(z_act, 1)

            def std(i, o):
                act.wait_ge(var_ok, 4 * i + o + 1)
                nc.scalar.activation(sd[o % 2], ve[o % 2], ACT.Sqrt).then_inc(std_ok, 1)

            def evac_h(i, o):
                b, r = 4 * i + o, o % 4
                if not (isinstance(b, int) and b < 2):
                    act.wait_ge(hmax_ok, b - 1)
                    act.wait_ge(h_stored[r % 2], 32 * i + 16 * (o // 2))
                for kt in range(HK):
                    act.wait_ge(tr_done, 4 * b + kt + 1)
                    nc.scalar.activation(hT[r % 2][:, kt, :], psum[:, ptr + kt, :], ACT.Identity,
                                         scale=col[r][:, kt:kt + 1], bias=col[r][:, 4 + kt:5 + kt]).then_inc(h_evac, 1)

            relu(0, 0)
            relu(0, 1)
            std(0, 0)
            for b in range(1, 3):
                relu(0, b + 1)
                std(0, b)
                evac_h(0, b - 1)
            with act.Fori(0, 3) as i:
                for o in range(3, 7):
                    relu(i, o + 1)
                    std(i, o)
                    evac_h(i, o - 1)
                    if o == 3:
                        w_upper(i)
            w_upper(NSL - 1)
            std(0, B - 1)
            evac_h(0, B - 2)
            evac_h(0, B - 1)

            def evac(n, m, uses, mm, red, stored, done):
                act.wait_ge(mm, n + 1)
                wait(act, red[m % 2], uses)
                wait(act, stored[m % 2], 16 * uses)
                nc.scalar.activation(raw[m % 2], half1[m % 2], ACT.Copy).then_inc(done[m % 2], 1)

            def gate_pair(i):
                for m in range(6):
                    evac(6 * i + m, m, 3 * i + m // 2, g_mm, g_red, g_stored, g_evac)
                    if m == 2:
                        w_upper(NSL + i)

            gate_pair(0)
            with act.Fori(1, B // 2) as i:
                gate_pair(i)

            def upper_h(j, s):
                nc.scalar.activation(a_hi[s], hq[:, bass.ds(j * TILE, TILE)], ACT.Copy).then_inc(hi2_ok, 1)

            act.wait_ge(g_mm, NCH)
            upper_h(0, 0)
            upper_h(1, 1)

            act.wait_ge(gma_ok, 2)
            nc.scalar.activation(k("fsig"), k("qf"), ACT.Sigmoid).then_inc(fsig_ok, 1)
            act.wait_ge(flag_ok, 1)
            flag = act.value_load(flag_sb[0:1, 0:1], min_val=0, max_val=1)

            def gate_sigmoid(n, p, uses, arrived, qdone, u_free, g_free, sdone):
                act.wait_ge(arrived[p], 16 * uses + 16)
                wait(act, g_free, n)
                nc.scalar.activation(gq, gin[p], ACT.Identity, scale=k("cq")).then_inc(qdone, 1)
                act.wait_ge(qdone, n + 1)
                wait(act, u_free, n)
                nc.scalar.activation(sig, gq, ACT.Sigmoid, scale=k("sg")).then_inc(sdone, 1)

            with act.If(flag > 0):
                for p in range(2):
                    gate_sigmoid(p, p, 0, f_in, f_q, f_u, f_f, f_sig)
                with act.Fori(1, NCH // 2) as i:
                    for p in range(2):
                        gate_sigmoid(2 * i + p, p, i, f_in, f_q, f_u, f_f, f_sig)
                act.wait_ge(f_max, 1)

            for p in range(2):
                act.wait_ge(g_stored[p], 16 * NCH // 2)
            def up_chunk(n, m, uses):
                gate_sigmoid(n, m % 2, uses, gin_in, gq_ok, su_ok, gg_ok, sig_ok)
                evac(n, m, uses, u_mm, u_red, u_stored, u_evac)
                act.wait_ge(u_evac[m % 2], uses + 1)
                wait(act, u_red[(m + 1) % 2], uses + m % 2)
                nc.scalar.activation(up_abs, raw[m % 2], ACT.Abs).then_inc(up_abs_ok, 1)

            def up_pair(i):
                for m in range(6):
                    up_chunk(6 * i + m, m, 3 * i + m // 2)
                    if m % CPB == 2:
                        upper_h(2 * i + m // CPB + 2, m // CPB)

            up_pair(0)
            with act.Fori(1, B // 2 - 1) as i:
                up_pair(i)
            for m in range(6):
                up_chunk(42 + m, m, 21 + m // 2)

            def quant_top(n, function):
                act.wait_ge(d_in, 32 * n + 32)
                nc.scalar.activation(u_top, p_top, function, scale=k("cu")).then_inc(d_uq, 1)

            def quant_up(p, arrived):
                act.wait_ge(e_in[p], arrived)
                nc.scalar.activation(uq[p], pin2[p], ACT.Identity, scale=k("cu")).then_inc(e_uq, 1)

            act.wait_ge(cu_ok, 1)
            quant_top(0, ACT.Abs)
            quant_up(0, 32)
            quant_up(1, 32)
            act.wait_ge(flag2_ok, 1)
            flag2 = act.value_load(flag2_sb[0:1, 0:1], min_val=0, max_val=1)
            with act.If(flag2 > 0):
                with act.Fori(0, NCH) as i:
                    quant_top(i + 1, ACT.Identity)

            def store_out(j, s, uses):
                act.wait_ge(res_ok[s], uses + 1)
                act.dma_start(out[bass.ds(j, 1)].rearrange("a (t p) h -> p (a t) h", p=P), osb[s]).then_inc(o_stored[s], 16)

            with act.Fori(0, B // 2 - 1) as i:
                for m in range(6):
                    act.wait_ge(e_oq, 6 * i + m + 1)
                    quant_up(m % 2, 32 * (3 * i + m // 2) + 64)
                    if m == 3:
                        store_out(2 * i, 0, i)
                store_out(2 * i + 1, 1, i)
            for m in range(4):
                act.wait_ge(e_oq, 42 + m + 1)
                quant_up(m % 2, 32 * (21 + m // 2) + 64)
            store_out(B - 2, 0, B // 2 - 1)
            store_out(B - 1, 1, B // 2 - 1)

        @block.vector
        def _(dve):
            count = [0]

            def link(ins):
                count[0] += 1
                ins.then_inc(kstep, 1)
                dve.wait_ge(kstep, count[0])

            V = nc.vector
            def block_maxima(group, m, n0):
                for part in range(3):
                    n = n0 + part
                    dve.wait_ge(nat_in[n % 2], 16 * (n // 2 + 1))
                    V.tensor_reduce(nat_m[group][:, m * NS + part * 64:m * NS + (part + 1) * 64],
                                    nat[group][n % 2].rearrange("p (b e) -> p b e", e=BLK), AX.X, ALU.max,
                                    apply_absolute_value=True).then_inc(nat_red, 1)

            def scales(group, m0, ms, reduced):
                mx, sc, tm, rc, sn = [a[group] for a in (nat_m, nat_s, nat_t, nat_r, nat_c)]
                dve.wait_ge(nat_red, reduced)
                link(V.tensor_scalar(sc, mx, 1.0 / QW, None, ALU.mult))
                link(V.scalar_tensor_tensor(tm, sc, -(QW + 1), mx, ALU.mult, ALU.add))
                link(V.tensor_tensor(tm, tm, sc, ALU.add))
                link(V.scalar_tensor_tensor(tm, tm, 1.0 / QW, sc, ALU.mult, ALU.add))
                link(V.tensor_scalar(sc, tm, TINY, None, ALU.max))
                V.tensor_reduce(k("smax%d" % m0, ms), sc.rearrange("p (m n) -> p m n", m=ms), AX.X, ALU.max).then_inc(smax_ok, 1)
                link(V.reciprocal(rc, sc))
                dve.wait_ge(sall_ok, group + 1)
                F, Fi = k("F%d" % m0, ms), k("Fi%d" % m0, ms)
                link(V.tensor_scalar(Fi.bitcast(I32), k("sall%d" % m0, ms).bitcast(I32), 0x7F800000, None, ALU.bitwise_and))
                link(V.reciprocal(F, Fi))
                link(V.tensor_scalar(F, F, W_TOP, None, ALU.mult))
                link(V.tensor_scalar(Fi, Fi, 1.0 / W_TOP, None, ALU.mult))
                for m in range(ms):
                    last = V.tensor_scalar(sn[:, m * NS:(m + 1) * NS], sc[:, m * NS:(m + 1) * NS],
                                           k("F%d" % (m0 + m)), None, ALU.mult)
                last.then_inc(scales_ok, 1)

            def w_quant(s):
                dve.wait_ge(prep_in, 144 * s + 144)
                V.tensor_tensor(pq, pw, pr, ALU.mult).then_inc(prep_q, 1)
                dve.wait_ge(prep_q, s + 1)
                V.tensor_tensor(pw, pq, ps_, ALU.mult).then_inc(prep_w, 1)

            dve.wait_ge(bias_in, 16)
            for part in range(PARTS):
                V.tensor_copy(bias_part[:, part, :], bias_rest[:, :]).then_inc(bias_step, 1)
                dve.wait_ge(bias_step, 2 * part + 1)
                last = V.tensor_tensor(bias_rest[:, :], bias_rest[:, :], bias_part[:, part, :], ALU.subtract)
                if part < PARTS - 1:
                    last.then_inc(bias_step, 1)
                    dve.wait_ge(bias_step, 2 * part + 2)
            last.then_inc(bias_ok, 1)

            def stats(i, o):
                b, s, r = 4 * i + o, o % 2, o % 4
                def add(t):
                    dve.wait_ge(y_done, 4 * b + t + 1)
                    V.tensor_tensor(xin[r][:, t, :], psum[:, py[t % 2], :], xin[r][:, t, :], ALU.add).then_inc(y_added, 1)

                def bn(t):
                    dve.wait_ge(y_added, 4 * b + t + 1)
                    V.bn_stats(bst[s][:, t, :], xin[r][:, t, :]).then_inc(bn_done, 1)

                add(0)
                add(1)
                bn(0)
                add(2)
                bn(1)
                add(3)
                bn(2)
                bn(3)
                dve.wait_ge(bn_done, 4 * b + 4)
                V.tensor_tensor(mu[s], bst[s][:, :, 1], bst[s][:, :, 4], ALU.add).then_inc(ag_done, 1)
                V.tensor_tensor(n1[s], bst[s][:, :, 1], bst[s][:, :, 4], ALU.subtract).then_inc(ag_done, 1)
                V.tensor_tensor(n2[s], bst[s][:, :, 2], bst[s][:, :, 5], ALU.add).then_inc(ag_done, 1)
                dve.wait_ge(ag_done, 6 * b + 2)
                V.scalar_tensor_tensor(rr[s], n1[s], 0.25, n1[s], ALU.mult, ALU.mult).then_inc(ag_done, 1)
                V.tensor_scalar(mv[s], mu[s], 0.5, None, ALU.mult).then_inc(ag_done, 1)
                dve.wait_ge(ag_done, 6 * b + 4)
                V.scalar_tensor_tensor(rs[s], n2[s], 1.0 / H, rr[s], ALU.mult, ALU.add).then_inc(ag_done, 1)
                dve.wait_ge(ag_done, 6 * b + 6)
                V.tensor_scalar(ve[s], rs[s], LN_EPS, None, ALU.add).then_inc(var_ok, 1)

            def norm(i, o):
                b, s, r = 4 * i + o, o % 2, o % 4
                dve.wait_ge(std_ok, b + 1)
                V.reciprocal(rs[s], sd[s]).then_inc(newton, 1)
                dve.wait_ge(newton, 4 * b + 1)
                V.scalar_tensor_tensor(n1[s], rs[s], -0.5, rs[s], ALU.mult, ALU.mult).then_inc(newton, 1)
                dve.wait_ge(newton, 4 * b + 2)
                V.tensor_tensor(n2[s], n1[s], ve[s], ALU.mult).then_inc(newton, 1)
                dve.wait_ge(newton, 4 * b + 3)
                V.scalar_tensor_tensor(rr[s], n2[s], 1.5, rs[s], ALU.add, ALU.mult).then_inc(newton, 1)
                dve.wait_ge(newton, 4 * b + 4)
                for t in range(ST):
                    last = V.tensor_scalar(xin[r][:, t, :], xin[r][:, t, :], mv[s][:, t:t + 1], rr[s][:, t:t + 1],
                                           ALU.subtract, ALU.mult)
                last.then_inc(yn_ok, 1)

            def reduce_h(i, o):
                b, s = 4 * i + o, o % 2
                dve.wait_ge(h_evac, 4 * b + 4)
                V.tensor_reduce(hmax[:, bass.ds(b, 1)], hT[s], AX.XY, ALU.max,
                                apply_absolute_value=True).then_inc(hmax_ok, 1)

            for b in range(2):
                stats(0, b)
                norm(0, b)
            block_maxima(0, 0, 0)
            scales(0, 0, 1, 3)
            stats(0, 2)
            reduce_h(0, 0)
            norm(0, 2)
            with dve.Fori(0, 3) as i:
                for o in range(3, 7):
                    stats(i, o)
                    reduce_h(i, o - 2)
                    norm(i, o)
                    if o == 3:
                        w_quant(i)
            w_quant(NSL - 1)
            stats(0, B - 1)
            reduce_h(0, B - 3)
            norm(0, B - 1)
            reduce_h(0, B - 2)
            reduce_h(0, B - 1)
            dve.wait_ge(hmax_ok, B)
            V.tensor_reduce(k("hm"), hmax[:, :], AX.X, ALU.max).then_inc(hm_ok, 1)
            dve.wait_ge(hma_ok, 1)
            link(V.tensor_scalar(k("sh"), k("hma"), 1.0 / QA, TINY, ALU.mult, ALU.max))
            link(V.reciprocal(k("rh"), k("sh")))

            def quant_h(j):
                dve.wait_ge(hin_in, 16 * j + 16)
                V.tensor_scalar(hq[:, bass.ds(j * TILE, TILE)], hin, k("rh"), None, ALU.mult).then_inc(hq_ok, 1)

            def split_h(j, s, mm, hi_done, done):
                wait(dve, mm, 3 * j - 3)
                V.tensor_scalar(a_hi[s], hq[:, bass.ds(j * TILE, TILE)], 1.0, None, ALU.mult).then_inc(hi_done, 1)
                dve.wait_ge(hi_done, j + 1)
                V.tensor_tensor(a_lo[s], hq[:, bass.ds(j * TILE, TILE)], a_hi[s], ALU.subtract).then_inc(done, 1)

            def reduce_gate(n, m, uses):
                dve.wait_ge(g_evac[m % 2], uses + 1)
                V.tensor_reduce(gmax[:, 0, bass.ds(n, 1)], raw[m % 2], AX.X, ALU.max, apply_absolute_value=True)
                V.tensor_reduce(gmax[:, 1, bass.ds(n, 1)], raw[m % 2], AX.X, ALU.max).then_inc(g_red[m % 2], 1)

            for j in range(2):
                quant_h(j)
                dve.wait_ge(hq_ok, j + 1)
                split_h(j, j, g_mm, hi_ok, split_ok)
            block_maxima(1, 0, 3)
            block_maxima(1, 1, 6)
            scales(1, 1, 2, 9)
            with dve.Fori(0, B // 2 - 1) as i:
                w_quant(NSL + i)
                for u in range(2):
                    for c in range(CPB):
                        m = CPB * u + c
                        reduce_gate(6 * i + m, m, 3 * i + m // 2)
                    quant_h(2 * i + u + 2)
                    dve.wait_ge(hq_ok, 2 * i + u + 3)
                    split_h(2 * i + u + 2, u, g_mm, hi_ok, split_ok)
            w_quant(3 * NSL - 1)
            for m in range(6):
                reduce_gate(42 + m, m, 21 + m // 2)

            for p in range(2):
                dve.wait_ge(g_red[p], NCH // 2)
            V.tensor_reduce(k("gm", 2), gmax[:, :, :], AX.X, ALU.max).then_inc(gm_ok, 1)

            def lower_h(j, s):
                dve.wait_ge(hi2_ok, j + 1)
                V.tensor_tensor(a_lo[s], hq[:, bass.ds(j * TILE, TILE)], a_hi[s], ALU.subtract).then_inc(split2_ok, 1)

            lower_h(0, 0)
            lower_h(1, 1)
            dve.wait_ge(gma_ok, 1)
            link(V.tensor_tensor(k("shg"), k("sh"), k("Fi0"), ALU.mult))
            link(V.tensor_tensor(k("gm"), k("gma"), k("shg"), ALU.mult))
            link(V.tensor_scalar(k("sg"), k("gm"), 1.0 / QA, TINY, ALU.mult, ALU.max))
            link(V.reciprocal(k("rg"), k("sg")))
            link(V.tensor_tensor(k("cq"), k("shg"), k("rg"), ALU.mult))
            link(V.tensor_tensor(flag_sb[:, :], k("gpa"), k("cq"), ALU.mult))
            V.tensor_tensor(k("qf"), flag_sb[:, :], k("sg"), ALU.mult).then_inc(gma_ok, 1)
            dve.wait_ge(fsig_ok, 1)
            link(V.tensor_scalar(k("fu").bitcast(I32), k("fsig"), SIGQ, SIGQ - 1, ALU.mult, ALU.min))
            link(V.scalar_tensor_tensor(k("fpos"), k("qf"), 1.0 / SIGQ, k("fu").bitcast(I32), ALU.mult, ALU.mult))
            V.tensor_scalar(flag_sb[:, :], k("fpos"), NEG_BOUND, None, ALU.is_lt).then_inc(flag_ok, 1)
            link(V.tensor_copy(k("fsel"), k("fpos")))

            def sig_u(n, sdone, udone):
                dve.wait_ge(sdone, n + 1)
                V.tensor_scalar(su16, sig, SIGQ, SIGQ - 1, ALU.mult, ALU.min).then_inc(udone, 1)
                dve.wait_ge(udone, n + 1)

            dve.wait_ge(flag_ok, 1)
            flag = dve.value_load(flag_sb[0:1, 0:1], min_val=0, max_val=1)
            with dve.If(flag > 0):
                def gate_max(n):
                    sig_u(n, f_sig, f_u)
                    wait(dve, f_red, n)
                    V.scalar_tensor_tensor(raw[1], gq, k("sg"), su16, ALU.mult, ALU.mult).then_inc(f_f, 1)
                    dve.wait_ge(f_f, n + 1)
                    V.tensor_reduce(fmax[:, bass.ds(n, 1)], raw[1], AX.X, ALU.max,
                                    apply_absolute_value=True).then_inc(f_red, 1)

                gate_max(0)
                with dve.Fori(1, NCH) as i:
                    gate_max(i)
                dve.wait_ge(f_red, NCH)
                V.tensor_reduce(k("fm"), fmax[:, :], AX.X, ALU.max).then_inc(f_max, 1)
                dve.wait_ge(f_all, 1)
                V.tensor_scalar(k("fsel"), k("fma"), 1.0 / SIGQ, None, ALU.mult).then_inc(f_max, 1)
                dve.wait_ge(f_max, 2)
            link(V.tensor_scalar(k("sf"), k("fsel"), 1.0 / QA, TINY, ALU.mult, ALU.max))
            link(V.reciprocal(k("rf"), k("sf")))
            link(V.tensor_scalar(k("sgn"), k("sg"), 1.0 / SIGQ, None, ALU.mult))
            link(V.tensor_tensor(k("cG"), k("sgn"), k("rf"), ALU.mult))

            def up_chunk(n, m, uses):
                h = m % 2
                sig_u(n, sig_ok, su_ok)
                wait(dve, gg_stored[h], 16 * uses)
                V.scalar_tensor_tensor(gg[h], gq, k("cG"), su16, ALU.mult, ALU.mult).then_inc(gg_ok, 1)
                dve.wait_ge(gg_ok, n + 1)
                dve.wait_ge(up_abs_ok, n + 1)
                V.tensor_reduce(umax[:, bass.ds(n, 1)], raw[h], AX.X, ALU.max, apply_absolute_value=True)
                V.tensor_tensor_reduce(up_abs, gg[h], up_abs, 1.0, 0.0, ALU.mult, ALU.max, gu_max[:, :]).then_inc(u_red[h], 1)
                dve.wait_ge(u_red[h], uses + 1)
                V.tensor_scalar(rmax[:, bass.ds(n, 1)], gu_max[:, :], 1.0, None, ALU.mult).then_inc(u_rmax, 1)

            def up_pair(i):
                for u in range(2):
                    for c in range(CPB):
                        m = CPB * u + c
                        up_chunk(6 * i + m, m, 3 * i + m // 2)
                    lower_h(2 * i + u + 2, u)

            up_pair(0)
            with dve.Fori(1, B // 2 - 1) as i:
                up_pair(i)
            for m in range(6):
                up_chunk(42 + m, m, 21 + m // 2)

            dve.wait_ge(u_rmax, NCH)
            V.tensor_reduce(rmax[:, NCH:NCH + 1], umax[:, :], AX.X, ALU.max).then_inc(um_ok, 1)
            dve.wait_ge(uma_ok, 1)
            link(V.max(top[:, :], rall[:, 0:NCH]))
            V.max_index(top_at[:, :], top[:, :], rall[:, 0:NCH]).then_inc(top_ok, 1)
            dve.wait_ge(top_ok, 1)
            link(V.tensor_tensor(k("shu"), k("sh"), k("Fi1"), ALU.mult))
            link(V.tensor_tensor(k("um"), rall[:, NCH:NCH + 1], k("shu"), ALU.mult))
            link(V.tensor_scalar(k("su"), k("um"), 1.0 / QA, TINY, ALU.mult, ALU.max))
            link(V.reciprocal(k("ru"), k("su")))
            V.tensor_tensor(k("cu"), k("shu"), k("ru"), ALU.mult).then_inc(cu_ok, 1)
            dve.wait_ge(cu_ok, 1)
            link(V.tensor_tensor(k("sfu"), k("sf"), k("su"), ALU.mult))

            link(V.tensor_scalar(k("nb"), k("rf"), NEG_BOUND, 0.5, ALU.mult, ALU.add))
            link(V.scalar_tensor_tensor(k("near"), rall[:, NCH:NCH + 1], k("nb"), top[:, 1:2], ALU.mult, ALU.max))
            link(V.tensor_scalar(k("gap"), k("near"), top[:, 0:1], k("cu"), ALU.subtract, ALU.mult))
            V.tensor_scalar(flag2_sb[:, :], k("gap"), MARGIN, None, ALU.is_ge).then_inc(flag2_ok, 1)
            dve.wait_ge(d_uq, 1)
            V.tensor_tensor_reduce(prod, g_top, u_top, 1.0, 0.0, ALU.mult, ALU.max, omax[:, NCH:NCH + 1]).then_inc(d_prod, 1)
            dve.wait_ge(flag2_ok, 1)
            flag2 = dve.value_load(flag2_sb[0:1, 0:1], min_val=0, max_val=1)
            with dve.If(flag2 > 0):
                def product(n):
                    dve.wait_ge(d_uq, n + 2)
                    V.tensor_tensor(prod, g_top, u_top, ALU.mult).then_inc(d_prod, 1)
                    dve.wait_ge(d_prod, n + 2)
                    V.tensor_reduce(omax[:, bass.ds(n, 1)], prod, AX.X, ALU.max,
                                    apply_absolute_value=True).then_inc(d_red, 1)
                    dve.wait_ge(d_red, n + 1)

                dve.wait_ge(d_prod, 1)
                with dve.Fori(0, NCH) as i:
                    product(i)
                V.tensor_reduce(omax[:, NCH:NCH + 1], omax[:, 0:NCH], AX.X, ALU.max).then_inc(d_red, 1)
                dve.wait_ge(d_red, NCH + 1)
            dve.wait_ge(d_prod, 1)
            V.tensor_copy(k("om"), omax[:, NCH:NCH + 1]).then_inc(om_ok, 1)
            dve.wait_ge(oma_ok, 1)
            link(V.tensor_tensor(k("om"), k("oma"), k("sfu"), ALU.mult))
            link(V.tensor_scalar(k("so"), k("om"), 1.0 / QA, TINY, ALU.mult, ALU.max))
            link(V.reciprocal(k("ro"), k("so")))
            link(V.tensor_tensor(k("cO"), k("sfu"), k("ro"), ALU.mult))
            link(V.tensor_tensor(k("cD"), k("so"), k("Fi2"), ALU.mult))

            def o_chunk(n, p, uses):
                dve.wait_ge(e_uq, n + 1)
                V.scalar_tensor_tensor(oq, gin2[p], k("cO"), uq[p], ALU.mult, ALU.mult).then_inc(e_oq, 1)
                dve.wait_ge(e_oq, n + 1)
                wait(dve, e_mm, n - 1)
                V.tensor_copy(o_hi[p], oq).then_inc(e_hi, 1)
                dve.wait_ge(e_hi, n + 1)
                V.tensor_tensor(o_lo[p], oq, o_hi[p], ALU.subtract).then_inc(e_split, 1)
                dve.wait_ge(e_split, n + 1)

            def residual(j, s, uses):
                dve.wait_ge(e_mm, 3 * j + 3)
                dve.wait_ge(x_in[s], 16 * uses + 16)
                wait(dve, o_stored[s], 16 * uses)
                V.scalar_tensor_tensor(osb[s].rearrange("p t h -> p (t h)"), half1[s], k("cD"),
                                       xres[s].rearrange("p t h -> p (t h)"), ALU.mult, ALU.add).then_inc(res_ok[s], 1)

            o_chunk(0, 0, 0)
            o_chunk(1, 1, 0)
            o_chunk(2, 0, 1)
            o_chunk(3, 1, 1)
            def down_pair(i):
                residual(2 * i, 0, i)
                for n in range(4, 7):
                    o_chunk(6 * i + n, n % 2, 3 * i + n // 2)
                residual(2 * i + 1, 1, i)
                for n in range(7, 10):
                    o_chunk(6 * i + n, n % 2, 3 * i + n // 2)

            down_pair(0)
            with dve.Fori(1, B // 2 - 1) as i:
                down_pair(i)
            residual(B - 2, 0, B // 2 - 1)
            o_chunk(46, 0, 23)
            o_chunk(47, 1, 23)
            residual(B - 1, 1, B // 2 - 1)

        @block.tensor
        def _(pe):
            T = nc.tensor

            def z_mm(i, o):
                b, s, r = 4 * i + o, o % 2, o % 4
                pe.wait_ge(in_a[r], 96 * (i + o // 4) + 96)
                if not (isinstance(b, int) and b < 2):
                    pe.wait_ge(z_act, b - 1)
                for kt in range(HK):
                    last = T.matmul(psum[:, pz[s], :], wdn[r][:, kt, :], xtin[r][:, kt, :],
                                    start=(kt == 0), stop=(kt == HK - 1))
                last.then_inc(z_done, 1)

            def y_mm(i, o):
                b, s, r = 4 * i + o, o % 2, o % 4
                pe.wait_ge(z_act, b + 1)
                for t in range(ST):
                    if not (isinstance(b, int) and 4 * b + t < 2):
                        pe.wait_ge(y_added, 4 * b + t - 1)
                    T.matmul(psum[:, py[t % 2], :], ones[:, :], bup[r], start=True, stop=False)
                    T.matmul(psum[:, py[t % 2], :], zsb[s][:, t * P:(t + 1) * P], wup[r],
                             start=False, stop=True).then_inc(y_done, 1)

            def transposes(i, o):
                b, r = 4 * i + o, o % 4
                pe.wait_ge(yn_ok, b + 1)
                for kt in range(HK):
                    if not (isinstance(b, int) and b < 1):
                        pe.wait_ge(h_evac, 4 * b + kt - 3)
                    for t in range(ST):
                        last = T.transpose(psum[:, ptr + kt, t * P:(t + 1) * P],
                                           xin[r][:, t, kt * P:(kt + 1) * P], ident[:, :])
                    last.then_inc(tr_done, 1)

            pe.wait_ge(const_ok, 3)
            z_mm(0, 0)
            z_mm(0, 1)
            y_mm(0, 0)
            for b in range(1, 3):
                z_mm(0, b + 1)
                y_mm(0, b)
                transposes(0, b - 1)
            with pe.Fori(0, 3) as i:
                for o in range(3, 7):
                    z_mm(i, o + 1)
                    y_mm(i, o)
                    transposes(i, o - 1)
            y_mm(0, B - 1)
            transposes(0, B - 2)
            transposes(0, B - 1)

            def ffn(matrix, split, evac, done):
                def pair_of_batches(i):
                    for u in range(2):
                        pe.wait_ge(split, 2 * i + u + 1)
                        for c in range(CPB):
                            m = CPB * u + c
                            wait(pe, evac[m % 2], 3 * i + m // 2)
                            for o in range(NB):
                                cs = (c * NB + o) * P
                                for kt in range(HK):
                                    hi = w_hi[:, matrix * NSL + kt, cs:cs + P]
                                    lo = w_lo[:, matrix * NSL + kt, cs:cs + P]
                                    ah, al = a_hi[u][:, kt * S:(kt + 1) * S], a_lo[u][:, kt * S:(kt + 1) * S]
                                    T.matmul(half[m % 2][:, o, :], hi, ah, start=(kt == 0), stop=False)
                                    T.matmul(half[m % 2][:, o, :], hi, al, start=False, stop=False)
                                    last = T.matmul(half[m % 2][:, o, :], lo, ah, start=False, stop=(kt == HK - 1))
                            last.then_inc(done, 1)

                pair_of_batches(0)
                with pe.Fori(1, B // 2) as i:
                    pair_of_batches(i)

            pe.wait_ge(prep_lo, NSL)
            pe.wait_ge(h_evac, 4 * B)
            ffn(0, split_ok, g_evac, g_mm)
            pe.wait_ge(prep_lo, 3 * NSL)
            for p in range(2):
                pe.wait_ge(g_evac[p], NCH // 2)
            ffn(1, split2_ok, u_evac, u_mm)

            for p in range(2):
                pe.wait_ge(u_evac[p], NCH // 2)
            def down_pair(i):
                for u in range(2):
                    wait(pe, res_ok[u], i)
                    for c in range(CPB):
                        m = CPB * u + c
                        pe.wait_ge(e_split, 6 * i + m + 1)
                        for t in range(ST):
                            for o in range(NB):
                                kt = c * NB + o
                                sl, at = 2 * NSL + kt // 3, (kt % 3) * H
                                hi, lo = w_hi[:, sl, at:at + H], w_lo[:, sl, at:at + H]
                                ts = slice(o * S + t * P, o * S + (t + 1) * P)
                                ah, al = o_hi[m % 2][:, ts], o_lo[m % 2][:, ts]
                                first, end = (c == 0 and o == 0), (c == CPB - 1 and o == NB - 1)
                                T.matmul(half[u][:, t, :], ah, hi, start=first, stop=False)
                                T.matmul(half[u][:, t, :], ah, lo, start=False, stop=False)
                                last = T.matmul(half[u][:, t, :], al, hi, start=False, stop=end)
                        last.then_inc(e_mm, 1)

            down_pair(0)
            with pe.Fori(1, B // 2) as i:
                down_pair(i)


def kernel(x, itok_B_0_6, L0_cond_down_w, L0_cond_down_b, L0_cond_up_w, L0_cond_up_b, L0_cond_ln_g,
           L0_cond_ln_b, L0_ffn_w_gate, L0_ffn_w_up, L0_ffn_w_down):
    import numpy as np
    import concourse.bacc as bacc
    from concourse.bass_utils import run_bass_kernel_spmd

    profiles = L0_cond_down_w.shape[0]

    def per_partition(v):
        return np.transpose(np.reshape(v, (profiles, HK, P)), (0, 2, 1))

    cols = np.concatenate([per_partition(L0_cond_ln_g), per_partition(L0_cond_ln_b),
                           np.reshape(L0_cond_down_b, (profiles, P, 1))], axis=2)

    def blocks_in(w):
        return np.reshape(np.transpose(np.reshape(w, (I, H // BLK, BLK)), (1, 0, 2)), (P, NS * BLK))

    def blocks_down(w):
        v = np.reshape(w, (H, NSL, 3, 4, BLK))
        return np.reshape(np.transpose(v, (1, 3, 2, 0, 4)), (P, NS * BLK))

    def slices_in(w):
        return np.reshape(np.transpose(w, (1, 0)), (NSL, P, SL))

    def slices_down(w):
        v = np.reshape(np.transpose(w, (1, 0)), (NSL, 3, P, H))
        return np.reshape(np.transpose(v, (0, 2, 1, 3)), (NSL, P, SL))

    arrays = {
        "x_in": x,
        "xT_in": np.transpose(x, (0, 2, 1)),
        "ids_in": np.reshape(itok_B_0_6, (1, B)),
        "down_w": L0_cond_down_w,
        "up_w": L0_cond_up_w,
        "up_b": L0_cond_up_b,
        "cols": cols,
        "w_blocks": np.stack([blocks_in(L0_ffn_w_gate), blocks_in(L0_ffn_w_up), blocks_down(L0_ffn_w_down)]),
        "w_slices": np.concatenate([slices_in(L0_ffn_w_gate), slices_in(L0_ffn_w_up), slices_down(L0_ffn_w_down)]),
    }
    arrays = {n: np.ascontiguousarray(a) for n, a in arrays.items()}
    nc = bacc.Bacc("TRN2", target_bir_lowering=False, num_devices=1)
    aps = [nc.dram_tensor(n, a.shape, mybir.dt.from_np(a.dtype), kind="ExternalInput").ap() for n, a in arrays.items()]
    out = nc.dram_tensor("out", (B, S, H), F32, kind="ExternalOutput").ap()
    adaln_ffn(nc, *aps, out)
    r = run_bass_kernel_spmd(nc, [arrays], core_ids=[0])
    return r.results[0]["out"]
```

```python
import concourse.bass as bass
from concourse import mybir
from contextlib import ExitStack

F32, F16, BF16 = mybir.dt.float32, mybir.dt.float16, mybir.dt.bfloat16
I16, U16, I32, U32 = mybir.dt.int16, mybir.dt.uint16, mybir.dt.int32, mybir.dt.uint32
ALU = mybir.AluOpType
ACT = mybir.ActivationFunctionType
AX = mybir.AxisListType

P = 128
B, S, H = 16, 512, 512
KB = 128
I = 1536
HK = H // P
ST = S // P
TILE = HK * S
NB = 4
CH = NB * S
CPB = I // P // NB
NCH = B * CPB
SL = 1536
NSL = 4
BLK = 32
NS = I * H // BLK // P
LN_EPS = 1e-5
QA = 32767.0
QW = 7.0
TINY = 1e-12
SIGQ = 65536.0
W_TOP = 4096.0
NEG_BOUND = 0.28
PARTS = 3
MARGIN = -36000.0


def adaln_ffn(nc, x, xT, ids, wd_dn, wu_dn, upb, cols, wnat, wtr, out):
    h_scr = nc.dram_tensor("h_scr", (B, P, TILE), F32).ap()
    s_scr = nc.dram_tensor("s_scr", (3, P, NS), F32).ap()
    r_scr = nc.dram_tensor("r_scr", (3, P, NS), F32).ap()
    gate_scr = nc.dram_tensor("gate_scr", (NCH, P, CH), F32).ap()
    up_scr = nc.dram_tensor("up_scr", (NCH, P, CH), F32).ap()
    b_scr = nc.dram_tensor("b_scr", (upb.shape[0], PARTS, H), BF16).ap()
    g_scr = nc.dram_tensor("g_scr", (NCH, P, CH), I16).ap()

    with ExitStack() as ctx:
        def sb(name, shape, dt):
            return ctx.enter_context(nc.sbuf_tensor(name, shape, dt))

        def sem(name):
            return ctx.enter_context(nc.semaphore(name))

        def pair(name):
            return [sem(name + "0"), sem(name + "1")]

        w_hi = sb("w_hi", [P, 3 * NSL, SL], F16)
        w_lo = sb("w_lo", [P, 3 * NSL, SL], F16)
        hq_mem = sb("hq_mem", [P, B * TILE // 2], F32)
        arena = sb("arena", [P, 15872], F32)
        ident = sb("ident", [P, P], F32)
        ones = sb("ones", [PARTS, P], BF16)
        n_prof = upb.shape[0]
        bias_rest = sb("bias_rest", [n_prof, H], F32)
        bias_part = sb("bias_part", [n_prof, PARTS, H], BF16)
        ids_sb = sb("ids_sb", [1, B], I32)
        flag_sb = sb("flag_sb", [P, 1], I32)
        hmax = sb("hmax", [P, B - 1 + HK], F32)
        gmax = sb("gmax", [P, 2, NCH], F32)
        umax = sb("umax", [P, NCH], F32)
        rmax = sb("rmax", [P, NCH + 1], F32)
        rall = sb("rall", [P, NCH + 1], F32)
        top = sb("top", [P, 8], F32)
        top_at = sb("top_at", [P, 8], U32)
        flag2_sb = sb("flag2_sb", [P, 1], I32)
        omax = sb("omax", [P, NCH + 1], F32)
        fmax = sb("fmax", [P, NCH], F32)
        K = sb("K", [P, 64], F32)
        gu_max = sb("gu_max", [P, 1], F32)

        def carve(mem, at, cols_, dt):
            size = 2 if dt in (F16, I16, U16, BF16) else 4
            v = mem[:, at // 4:(at + cols_ * size) // 4]
            return v if dt == F32 else v.bitcast(dt)

        hq = hq_mem[:, :].bitcast(I16)

        pw, pr, ps_ = [carve(arena, a, SL, F32) for a in (0, 6144, 12288)]
        pq = carve(arena, 18432, SL, I16)
        def mem3(mem, at, a, b):
            return carve(mem, at, a * b, F32).rearrange("p (a b) -> p a b", a=a)
        wm1 = w_hi[:, NSL:, :].rearrange("p a b -> p (a b)").bitcast(F32)
        wm2 = w_lo[:, NSL:, :].rearrange("p a b -> p (a b)").bitcast(F32)
        R4 = range(4)
        nat = [[carve(arena, 21504 + p * 8192, 2048, F32) for p in range(3)],
               [carve(wm1, p * 8192, 2048, F32) for p in range(3)]]

        def small(mem, at, m):
            return [carve(mem, at + k * m * NS * 4, m * NS, F32) for k in range(5)]
        nat_m, nat_s, nat_t, nat_r, nat_c = zip(small(arena, 46080, 1), small(wm2, 0, 2))
        xin = [mem3(hq_mem, p * 8192, ST, H) for p in R4]
        xtin = [mem3(hq_mem, 32768 + p * 8192, HK, S) for p in R4]
        wdn = [mem3(wm1, p * 2048, HK, KB) for p in R4]
        wup = [carve(wm1, 8192 + p * 2048, H, F32) for p in R4]
        bup = [wm1[0:PARTS, (16384 + p * 1024) // 4:(17408 + p * 1024) // 4].bitcast(BF16) for p in R4]
        zsb = [carve(wm2, p * 2048, S, F32) for p in range(2)]
        hT = [mem3(wm2, 4096 + p * 8192, HK, S) for p in range(2)]
        col = [carve(wm2, 20480 + p * 64, 9, F32) for p in R4]
        bst = [mem3(wm2, 20736 + p * 128, ST, 6) for p in range(2)]
        mu, mv, ve, sd, rs, n1, n2, rr = [[carve(wm2, 20992 + n * 32 + p * 16, ST, F32) for p in range(2)]
                                          for n in range(8)]

        hin = carve(arena, 21504, TILE, F32)
        a_hi = [carve(arena, 29696 + p * 4096, TILE, F16) for p in range(2)]
        a_lo = [carve(arena, 37888 + p * 4096, TILE, F16) for p in range(2)]
        raw = [carve(arena, 46080 + p * 8192, CH, F32) for p in range(2)]
        assert 46080 + 16384 <= 15872 * 4
        gin = [carve(arena, p * 8192, CH, F32) for p in range(2)]
        wg1 = w_hi[:, 0:NSL, :].rearrange("p a b -> p (a b)").bitcast(F32)
        wg2 = w_lo[:, 0:NSL, :].rearrange("p a b -> p (a b)").bitcast(F32)
        su16 = carve(arena, 20480, CH, U16)
        gg = [carve(arena, 24576, CH, I16), carve(wg1, 8192, CH, I16)]
        up_abs = carve(wg1, 0, CH, F32)
        sig = carve(wg2, 0, CH, F32)
        gq = carve(wg2, 8192, CH, I16)

        gin2 = [carve(arena, p * 4096, CH, I16) for p in range(2)]
        pin2 = [carve(arena, 8192 + p * 8192, CH, F32) for p in range(2)]
        uq = [carve(arena, 24576 + p * 4096, CH, I16) for p in range(2)]
        g_top, u_top = [carve(hq_mem, 49152 + p * 4096, CH, I16) for p in range(2)]
        p_top = carve(hq_mem, 57344, CH, F32)
        prod = carve(arena, 32768, CH, F32)
        oq = carve(arena, 40960, CH, I16)
        o_hi = [carve(hq_mem, p * 4096, CH, F16) for p in range(2)]
        o_lo = [carve(hq_mem, 8192 + p * 4096, CH, F16) for p in range(2)]
        xres = [mem3(hq_mem, 16384 + p * 8192, ST, H) for p in range(2)]
        osb = [mem3(hq_mem, 32768 + p * 8192, ST, H) for p in range(2)]

        psum = ctx.enter_context(nc.psum_tensor("psum", [P, 8, 512], F32))
        half = [psum[:, 4 * p:4 * p + 4, :] for p in range(2)]
        half1 = [h.rearrange("p a n -> p (a n)") for h in half]
        pz, py, ptr = [0, 1], [2, 3], 4

        names = ("smax0 smax1 smax2 sall0 sall1 sall2 F0 F1 F2 Fi0 Fi1 Fi2 hm hma sh rh "
                 "gm gp gma gpa shg sg rg cq qf fsig fu fpos fm fma fsel sf rf cG sgn um uma shu su ru cu "
                 "om oma sfu so ro cO cD gap nb near").split()

        def k(n, w=1):
            a = names.index(n)
            return K[:, a:a + w]

        ids_in = sem("ids_in")
        const_ok = sem("const_ok")
        kstep = sem("kstep")
        nat_in, nat_red = [sem("nat_in%d" % p) for p in range(3)], sem("nat_red")
        bias_in, bias_step, bias_ok, bias_out = sem("bias_in"), sem("bias_step"), sem("bias_ok"), sem("bias_out")
        smax_ok, sall_ok = sem("smax_ok"), sem("sall_ok")
        scales_ok, scr_out = sem("scales_ok"), sem("scr_out")
        prep_in, prep_q = sem("prep_in"), sem("prep_q")
        prep_w, prep_hi, prep_lo = sem("prep_w"), sem("prep_hi"), sem("prep_lo")
        in_z, in_c, in_y, in_x = [[sem("in_%s%d" % (v, p)) for p in range(4)] for v in "zcyx"]
        z_done, z_act, y_done, y_added = sem("z_done"), sem("z_act"), sem("y_done"), sem("y_added")
        bn_done, ag_done, var_ok, std_ok = sem("bn_done"), sem("ag_done"), sem("var_ok"), sem("std_ok")
        newton, yn_ok, tr_done, h_evac = sem("newton"), sem("yn_ok"), sem("tr_done"), sem("h_evac")
        hmax_ok, h_stored = sem("hmax_ok"), pair("h_stored")
        hm_ok, hma_ok = sem("hm_ok"), sem("hma_ok")
        hin_in, hq_ok, hi_ok, split_ok = sem("hin_in"), sem("hq_ok"), sem("hi_ok"), sem("split_ok")
        g_mm, g_evac, g_red, g_stored = sem("g_mm"), pair("g_evac"), pair("g_red"), pair("g_stored")
        gm_ok, gma_ok, fsig_ok, flag_ok = sem("gm_ok"), sem("gma_ok"), sem("fsig_ok"), sem("flag_ok")
        f_in, f_q, f_sig, f_u, f_f = pair("f_in"), sem("f_q"), sem("f_sig"), sem("f_u"), sem("f_f")
        f_red, f_max, f_all, cg_ok = sem("f_red"), sem("f_max"), sem("f_all"), sem("cg_ok")
        hi2_ok, split2_ok = sem("hi2_ok"), sem("split2_ok")
        u_mm, u_evac, u_red, u_stored = sem("u_mm"), pair("u_evac"), pair("u_red"), pair("u_stored")
        gin_in, gq_ok, sig_ok, su_ok = pair("gin_in"), sem("gq_ok"), sem("sig_ok"), sem("su_ok")
        gg_ok, gg_stored = sem("gg_ok"), pair("gg_stored")
        um_ok, uma_ok, top_ok, cu_ok, flag2_ok = sem("um_ok"), sem("uma_ok"), sem("top_ok"), sem("cu_ok"), sem("flag2_ok")
        up_abs_ok, u_rmax = sem("up_abs_ok"), sem("u_rmax")
        d_in, d_uq, d_prod, d_red = sem("d_in"), sem("d_uq"), sem("d_prod"), sem("d_red")
        om_ok, oma_ok = sem("om_ok"), sem("oma_ok")
        e_in, e_uq, e_oq, e_hi, e_split = pair("e_in"), sem("e_uq"), sem("e_oq"), sem("e_hi"), sem("e_split")
        e_mm, e_tile, x_in, res_ok, o_stored = sem("e_mm"), sem("e_tile"), pair("x_in"), pair("res_ok"), pair("o_stored")

        def wait(engine, semaphore, value):
            if not (isinstance(value, int) and value <= 0):
                engine.wait_ge(semaphore, value)

        block = ctx.enter_context(nc.Block())

        @block.sync
        def _(sp):
            sp.dma_start(ids_sb[:, :], ids).then_inc(ids_in, 16)
            sp.dma_start(bias_rest[:, :], upb).then_inc(bias_in, 16)

            def load_blocks(group, m):
                for part in range(3):
                    if m == 2:
                        sp.wait_ge(nat_red, 3 + part + 1)
                    sp.dma_start(nat[group][part], wnat[m, :, part * 2048:(part + 1) * 2048]).then_inc(nat_in[part], 16)

            s_rows = s_scr.rearrange("m p n -> (m p n)").rearrange("(s q c) -> s q c", q=4, c=SL)
            r_rows = r_scr.rearrange("m p n -> (m p n)").rearrange("(s q c) -> s q c", q=4, c=SL)

            def spill_scales(group, ms, done):
                sp.wait_ge(scales_ok, group + 1)
                for n, m in enumerate(ms):
                    for scr, src in ((s_scr, nat_c), (r_scr, nat_r)):
                        sp.dma_start(scr[m], src[group][:, n * NS:(n + 1) * NS]).then_inc(scr_out, 16)
                sp.wait_ge(scr_out, done)

            def load_slice(s):
                sp.dma_start(pw, wtr[bass.ds(s, 1)].rearrange("a p n -> p (a n)")).then_inc(prep_in, 16)
                for q in range(4):
                    for dst, rows in ((ps_, s_rows), (pr, r_rows)):
                        src = rows[bass.ds(s, 1), q, :].partition_broadcast(BLK)
                        sp.dma_start(dst[32 * q:32 * q + 32, :], src.rearrange("r a n -> r (a n)")).then_inc(prep_in, 16)

            sp.wait_ge(ids_in, 16)

            def profile(b):
                return sp.value_load(ids_sb[0:1, bass.ds(b, 1)], min_val=0, max_val=n_prof - 1)

            def load_z(b, s):
                p = profile(b)
                sp.dma_start(xtin[s], xT[bass.ds(b, 1)].rearrange("a (k p) t -> p (a k) t", p=P)).then_inc(in_z[s], 16)
                sp.dma_start(wdn[s], wd_dn[bass.ds(p, 1)].rearrange("a (k p) n -> p (a k) n", p=P)).then_inc(in_z[s], 16)

            def load_col(b, s):
                p = profile(b)
                sp.dma_start(col[s], cols[bass.ds(p, 1)].rearrange("a p n -> p (a n)")).then_inc(in_c[s], 16)

            def load_y(b, s, first=False):
                p = profile(b)
                sp.dma_start(wup[s], wu_dn[bass.ds(p, 1)].rearrange("a p n -> p (a n)")).then_inc(in_y[s], 16)
                if first:
                    sp.wait_ge(bias_ok, 1)
                    sp.dma_start(b_scr, bias_part[:, :, :]).then_inc(bias_out, 16)
                    sp.wait_ge(bias_out, 16)
                sp.dma_start(bup[s], b_scr[bass.ds(p, 1)].rearrange("a r n -> (a r) n")).then_inc(in_y[s], 16)

            def load_x_in(b, s):
                sp.dma_start(xin[s], x[bass.ds(b, 1)].rearrange("a (t p) h -> p (a t) h", p=P)).then_inc(in_x[s], 16)

            def store_h(b, s):
                sp.dma_start(h_scr[bass.ds(b, 1)].rearrange("a p n -> p (a n)"),
                             hT[s].rearrange("p k n -> p (k n)")).then_inc(h_stored[s], 16)

            def step(b, r, x_left=True, y_left=True, z_left=True):
                sp.wait_ge(h_evac, 4 * b + 4)
                store_h(b, r % 2)
                if x_left:
                    load_col(b + 4, r)
                    load_x_in(b + 4, r)
                if y_left:
                    load_y(b + 5, (r + 1) % 4)
                if z_left:
                    load_z(b + 6, (r + 2) % 4)

            def slice_part(s, part):
                if part == 0:
                    sp.dma_start(pw, wtr[bass.ds(s, 1)].rearrange("a p n -> p (a n)")).then_inc(prep_in, 16)
                for q in ((), (0, 1), (2, 3))[part]:
                    for dst, rows in ((ps_, s_rows), (pr, r_rows)):
                        src = rows[bass.ds(s, 1), q, :].partition_broadcast(BLK)
                        sp.dma_start(dst[32 * q:32 * q + 32, :], src.rearrange("r a n -> r (a n)")).then_inc(prep_in, 16)

            def load_slice(s):
                for part in range(3):
                    slice_part(s, part)

            load_z(0, 0)
            load_col(0, 0)
            load_z(1, 1)
            load_y(0, 0, True)
            load_x_in(0, 0)
            load_col(1, 1)
            load_y(1, 1)
            load_x_in(1, 1)
            load_z(2, 2)
            load_col(2, 2)
            load_z(3, 3)
            load_blocks(0, 0)
            load_x_in(2, 2)
            load_y(2, 2)
            load_y(3, 3)
            load_col(3, 3)
            load_x_in(3, 3)
            sp.wait_ge(z_act, 1)
            load_z(4, 0)
            sp.wait_ge(z_act, 2)
            load_z(5, 1)
            sp.wait_ge(y_done, 4)
            load_y(4, 0)
            step(0, 0)
            step(1, 1)
            spill_scales(0, [0], 32)
            slice_part(0, 0)
            slice_part(0, 1)
            with sp.Fori(0, 2) as i:
                step(4 * i + 2, 2)
                slice_part(i, 2)
                step(4 * i + 3, 3)
                step(4 * i + 4, 0)
                sp.wait_ge(prep_lo, i + 1)
                slice_part(i + 1, 0)
                step(4 * i + 5, 1)
                slice_part(i + 1, 1)
            step(10, 2, z_left=False)
            slice_part(2, 2)
            step(11, 3, z_left=False, y_left=False)
            step(12, 0, z_left=False, y_left=False, x_left=False)
            sp.wait_ge(prep_lo, 3)
            load_slice(3)
            step(13, 1, z_left=False, y_left=False, x_left=False)

            sp.wait_ge(y_done, 4 * B)

            sp.wait_ge(h_stored[0], 16 * (B // 2 - 1))
            sp.wait_ge(h_stored[1], 16 * (B // 2 - 1))

            def load_h(j):
                sp.dma_start(hin, h_scr[bass.ds(j - 2, 1)].rearrange("a p n -> p (a n)")).then_inc(hin_in, 16)

            def store_raw(n, m, evac, scr, stored, uses):
                sp.wait_ge(evac[m % 2], uses + 1)
                sp.dma_start(scr[bass.ds(n, 1)].rearrange("a p n -> p (a n)"), raw[m % 2]).then_inc(stored[m % 2], 16)

            def gate_pair(i, first=False, last=False):
                for m in range(6):
                    store_raw(6 * i + m, m, g_evac, gate_scr, g_stored, 3 * i + m // 2)
                    if m % CPB == 0 and not last:
                        j = 2 * i + m // CPB + 2
                        sp.wait_ge(hq_ok, j)
                        load_h(j)
                    if m == 0 and first:
                        load_blocks(1, 2)
                    if m == 3 and first:
                        spill_scales(1, [1, 2], 96)
                        load_slice(NSL)
                    if m == 2 and not first:
                        sp.wait_ge(prep_lo, NSL + i)
                        load_slice(NSL + i)

            load_blocks(1, 1)
            gate_pair(0, first=True)
            with sp.Fori(1, B // 2 - 1) as i:
                gate_pair(i)
            gate_pair(B // 2 - 1, last=True)
            sp.wait_ge(g_stored[0], 16 * NCH // 2)
            sp.wait_ge(g_stored[1], 16 * NCH // 2)
            sp.wait_ge(prep_lo, 3 * NSL)

            def load_gate(n, p, done):
                sp.dma_start(gin[p], gate_scr[bass.ds(n, 1)].rearrange("a p n -> p (a n)")).then_inc(done[p], 16)

            sp.wait_ge(flag_ok, 1)
            flag = sp.value_load(flag_sb[0:1, 0:1], min_val=0, max_val=1)
            with sp.If(flag > 0):
                load_gate(0, 0, f_in)
                load_gate(1, 1, f_in)
                with sp.Fori(1, NCH // 2) as i:
                    for p in range(2):
                        sp.wait_ge(f_q, 2 * i + p - 1)
                        load_gate(2 * i + p, p, f_in)
                sp.wait_ge(f_q, NCH)
            load_gate(0, 0, gin_in)
            load_gate(1, 1, gin_in)

            def up_chunk(n, m, uses, last):
                store_raw(n, m, u_evac, up_scr, u_stored, uses)
                sp.wait_ge(gg_ok, n + 1)
                if not last:
                    load_gate(n + 2, m % 2, gin_in)
                sp.dma_start(g_scr[bass.ds(n, 1)].rearrange("a p n -> p (a n)"), gg[m % 2]).then_inc(gg_stored[m % 2], 16)

            with sp.Fori(0, B // 2 - 1) as i:
                for m in range(6):
                    up_chunk(6 * i + m, m, 3 * i + m // 2, False)
            for m in range(6):
                up_chunk(42 + m, m, 21 + m // 2, m >= 4)
            for p in range(2):
                sp.wait_ge(u_stored[p], 16 * NCH // 2)
                sp.wait_ge(gg_stored[p], 16 * NCH // 2)

            def load_top(n):
                sp.dma_start(p_top, up_scr[bass.ds(n, 1)].rearrange("a p n -> p (a n)")).then_inc(d_in, 16)
                sp.dma_start(g_top, g_scr[bass.ds(n, 1)].rearrange("a p n -> p (a n)")).then_inc(d_in, 16)

            def load_gu(n, p, done):
                sp.dma_start(gin2[p], g_scr[bass.ds(n, 1)].rearrange("a p n -> p (a n)")).then_inc(done[p], 16)
                sp.dma_start(pin2[p], up_scr[bass.ds(n, 1)].rearrange("a p n -> p (a n)")).then_inc(done[p], 16)

            sp.wait_ge(top_ok, 1)
            load_top(sp.value_load(top_at[0:1, 0:1], min_val=0, max_val=NCH - 1))
            load_gu(0, 0, e_in)
            load_gu(1, 1, e_in)
            sp.wait_ge(flag2_ok, 1)
            flag2 = sp.value_load(flag2_sb[0:1, 0:1], min_val=0, max_val=1)
            with sp.If(flag2 > 0):
                with sp.Fori(0, NCH) as i:
                    sp.wait_ge(d_prod, i + 1)
                    load_top(i)

            def load_x(batch, s):
                sp.dma_start(xres[s], x[bass.ds(batch, 1)].rearrange("a (t p) h -> p (a t) h", p=P)).then_inc(x_in[s], 16)

            load_x(B - 2, 0)
            load_x(B - 1, 1)
            with sp.Fori(0, B // 2 - 1) as i:
                for m in range(6):
                    sp.wait_ge(e_oq, 6 * i + m + 1)
                    load_gu(6 * i + m + 2, m % 2, e_in)
                    if m == 4:
                        sp.wait_ge(res_ok[0], i + 1)
                        load_x(2 * i, 0)
                sp.wait_ge(res_ok[1], i + 1)
                load_x(2 * i + 1, 1)
            for m in range(4):
                sp.wait_ge(e_oq, 42 + m + 1)
                load_gu(42 + m + 2, m % 2, e_in)
            sp.wait_ge(o_stored[0], 16 * B // 2)
            sp.wait_ge(o_stored[1], 16 * (B // 2 - 1 + ST))

        @block.gpsimd
        def _(pool):
            RMAX = bass.bass_isa.ReduceOp.max
            nc.gpsimd.memset(ident[:, :], 0.0).then_inc(const_ok, 1)
            nc.gpsimd.memset(ones[:, :], 1.0).then_inc(const_ok, 1)
            pool.wait_ge(const_ok, 2)
            nc.gpsimd.affine_select(out=ident[:, :], in_=ident[:, :], compare_op=ALU.not_equal, fill=1.0,
                                    base=0, pattern=[[-1, P]], channel_multiplier=1).then_inc(const_ok, 1)

            def all_max(after, count, src, dst, done):
                pool.wait_ge(after, count)
                nc.gpsimd.partition_all_reduce(dst, src, P, RMAX).then_inc(done, 1)

            def w_lower(s):
                pool.wait_ge(prep_hi, s + 1)
                nc.gpsimd.tensor_tensor(w_lo[:, bass.ds(s, 1), :].rearrange("p a n -> p (a n)"), pw,
                                        w_hi[:, bass.ds(s, 1), :].rearrange("p a n -> p (a n)"),
                                        ALU.subtract).then_inc(prep_lo, 1)

            all_max(smax_ok, 1, k("smax0"), k("sall0"), sall_ok)
            with pool.Fori(0, NSL) as i:
                w_lower(i)
            all_max(hm_ok, 1, k("hm"), k("hma"), hma_ok)
            all_max(smax_ok, 2, k("smax1", 2), k("sall1", 2), sall_ok)
            with pool.Fori(0, 2 * NSL) as i:
                w_lower(NSL + i)
            all_max(gm_ok, 1, k("gm", 2), k("gma", 2), gma_ok)
            pool.wait_ge(flag_ok, 1)
            flag = pool.value_load(flag_sb[0:1, 0:1], min_val=0, max_val=1)
            with pool.If(flag > 0):
                all_max(f_max, 1, k("fm"), k("fma"), f_all)
            all_max(um_ok, 1, rmax[:, :], rall[:, :], uma_ok)
            all_max(om_ok, 1, k("om"), k("oma"), oma_ok)

        @block.scalar
        def _(act):
            def w_upper(s):
                act.wait_ge(prep_w, s + 1)
                nc.scalar.activation(w_hi[:, bass.ds(s, 1), :].rearrange("p a n -> p (a n)"), pw,
                                     ACT.Copy).then_inc(prep_hi, 1)

            def relu(i, o):
                b, r = 4 * i + o, o % 4
                act.wait_ge(in_c[r], 16 * (i + o // 4) + 16)
                act.wait_ge(z_done, b + 1)
                if not (isinstance(b, int) and b < 2):
                    act.wait_ge(y_done, 4 * b - 4)
                nc.scalar.activation(zsb[r % 2], psum[:, pz[r % 2], :], ACT.Relu, bias=col[r][:, 8:9]).then_inc(z_act, 1)

            def std(i, o):
                act.wait_ge(var_ok, 4 * i + o + 1)
                nc.scalar.activation(sd[o % 2], ve[o % 2], ACT.Sqrt).then_inc(std_ok, 1)

            def evac_h(i, o):
                b, r = 4 * i + o, o % 4
                if not (isinstance(b, int) and b < 2):
                    act.wait_ge(hmax_ok, b - 1)
                    act.wait_ge(h_stored[r % 2], 32 * i + 16 * (o // 2))
                for kt in range(HK):
                    act.wait_ge(tr_done, 4 * b + kt + 1)
                    nc.scalar.activation(hT[r % 2][:, kt, :], psum[:, ptr + kt, :], ACT.Identity,
                                         scale=col[r][:, kt:kt + 1], bias=col[r][:, 4 + kt:5 + kt]).then_inc(h_evac, 1)

            relu(0, 0)
            relu(0, 1)
            std(0, 0)
            for b in range(1, 3):
                relu(0, b + 1)
                std(0, b)
                evac_h(0, b - 1)
            with act.Fori(0, 3) as i:
                for o in range(3, 7):
                    relu(i, o + 1)
                    std(i, o)
                    evac_h(i, o - 1)
                    if o == 4:
                        w_upper(i)
            w_upper(NSL - 1)
            std(0, B - 1)
            evac_h(0, B - 2)
            evac_h(0, B - 1)

            def evac(n, m, uses, mm, red, stored, done):
                act.wait_ge(mm, n + 1)
                wait(act, red[m % 2], uses)
                wait(act, stored[m % 2], 16 * uses)
                nc.scalar.activation(raw[m % 2], half1[m % 2], ACT.Copy).then_inc(done[m % 2], 1)

            def gate_pair(i):
                for m in range(6):
                    evac(6 * i + m, m, 3 * i + m // 2, g_mm, g_red, g_stored, g_evac)
                w_upper(NSL + i)

            gate_pair(0)
            with act.Fori(1, B // 2) as i:
                gate_pair(i)

            def upper_h(j, s):
                nc.scalar.activation(a_hi[s], hq[:, bass.ds(j * TILE, TILE)], ACT.Copy).then_inc(hi2_ok, 1)

            act.wait_ge(g_mm, NCH)
            upper_h(0, 0)
            upper_h(1, 1)

            act.wait_ge(gma_ok, 2)
            nc.scalar.activation(k("fsig"), k("qf"), ACT.Sigmoid).then_inc(fsig_ok, 1)
            act.wait_ge(flag_ok, 1)
            flag = act.value_load(flag_sb[0:1, 0:1], min_val=0, max_val=1)

            def gate_sigmoid(n, p, uses, arrived, qdone, u_free, g_free, sdone):
                act.wait_ge(arrived[p], 16 * uses + 16)
                wait(act, g_free, n)
                nc.scalar.activation(gq, gin[p], ACT.Identity, scale=k("cq")).then_inc(qdone, 1)
                act.wait_ge(qdone, n + 1)
                wait(act, u_free, n)
                nc.scalar.activation(sig, gq, ACT.Sigmoid, scale=k("sg")).then_inc(sdone, 1)

            with act.If(flag > 0):
                for p in range(2):
                    gate_sigmoid(p, p, 0, f_in, f_q, f_u, f_f, f_sig)
                with act.Fori(1, NCH // 2) as i:
                    for p in range(2):
                        gate_sigmoid(2 * i + p, p, i, f_in, f_q, f_u, f_f, f_sig)
                act.wait_ge(f_max, 1)

            for p in range(2):
                act.wait_ge(g_stored[p], 16 * NCH // 2)
            def up_chunk(n, m, uses):
                gate_sigmoid(n, m % 2, uses, gin_in, gq_ok, su_ok, gg_ok, sig_ok)
                evac(n, m, uses, u_mm, u_red, u_stored, u_evac)
                act.wait_ge(u_evac[m % 2], uses + 1)
                wait(act, u_red[(m + 1) % 2], uses + m % 2)
                nc.scalar.activation(up_abs, raw[m % 2], ACT.Abs).then_inc(up_abs_ok, 1)

            def up_pair(i):
                for m in range(6):
                    up_chunk(6 * i + m, m, 3 * i + m // 2)
                    if m % CPB == 2:
                        upper_h(2 * i + m // CPB + 2, m // CPB)

            up_pair(0)
            with act.Fori(1, B // 2 - 1) as i:
                up_pair(i)
            for m in range(6):
                up_chunk(42 + m, m, 21 + m // 2)

            def quant_top(n, function):
                act.wait_ge(d_in, 32 * n + 32)
                nc.scalar.activation(u_top, p_top, function, scale=k("cu")).then_inc(d_uq, 1)

            def quant_up(p, arrived):
                act.wait_ge(e_in[p], arrived)
                nc.scalar.activation(uq[p], pin2[p], ACT.Identity, scale=k("cu")).then_inc(e_uq, 1)

            act.wait_ge(cu_ok, 1)
            quant_top(0, ACT.Abs)
            quant_up(0, 32)
            quant_up(1, 32)
            act.wait_ge(flag2_ok, 1)
            flag2 = act.value_load(flag2_sb[0:1, 0:1], min_val=0, max_val=1)
            with act.If(flag2 > 0):
                with act.Fori(0, NCH) as i:
                    quant_top(i + 1, ACT.Identity)

            def store_out(batch, s, uses):
                act.wait_ge(res_ok[s], uses + 1)
                act.dma_start(out[bass.ds(batch, 1)].rearrange("a (t p) h -> p (a t) h", p=P), osb[s]).then_inc(o_stored[s], 16)

            def down_pair(i, batch):
                for m in range(6):
                    act.wait_ge(e_oq, 6 * i + m + 1)
                    quant_up(m % 2, 32 * (3 * i + m // 2) + 64)
                    if m == 3:
                        store_out(batch, 0, i)
                store_out(batch + 1, 1, i)

            down_pair(0, B - 2)
            with act.Fori(1, B // 2 - 1) as i:
                down_pair(i, 2 * i - 2)
            for m in range(4):
                act.wait_ge(e_oq, 42 + m + 1)
                quant_up(m % 2, 32 * (21 + m // 2) + 64)
            store_out(B - 4, 0, B // 2 - 1)
            for t in range(ST):
                act.wait_ge(res_ok[1], B // 2 - 1 + t + 1)
                act.dma_start(out[B - 3, t * P:(t + 1) * P, :], osb[1][:, t, :]).then_inc(o_stored[1], 16)

        @block.vector
        def _(dve):
            count = [0]

            def link(ins):
                count[0] += 1
                ins.then_inc(kstep, 1)
                dve.wait_ge(kstep, count[0])

            V = nc.vector
            def block_maxima(group, m, part):
                dve.wait_ge(nat_in[part], 16 * (group + m) + 16)
                V.tensor_reduce(nat_m[group][:, m * NS + part * 64:m * NS + (part + 1) * 64],
                                nat[group][part].rearrange("p (b e) -> p b e", e=BLK), AX.X, ALU.max,
                                apply_absolute_value=True).then_inc(nat_red, 1)

            def scales(group, m0, ms, reduced):
                mx, sc, tm, rc, sn = [a[group] for a in (nat_m, nat_s, nat_t, nat_r, nat_c)]
                dve.wait_ge(nat_red, reduced)
                link(V.tensor_scalar(sc, mx, 1.0 / QW, None, ALU.mult))
                link(V.scalar_tensor_tensor(tm, sc, -(QW + 1), mx, ALU.mult, ALU.add))
                link(V.tensor_tensor(tm, tm, sc, ALU.add))
                link(V.scalar_tensor_tensor(tm, tm, 1.0 / QW, sc, ALU.mult, ALU.add))
                link(V.tensor_scalar(sc, tm, TINY, None, ALU.max))
                V.tensor_reduce(k("smax%d" % m0, ms), sc.rearrange("p (m n) -> p m n", m=ms), AX.X, ALU.max).then_inc(smax_ok, 1)
                link(V.reciprocal(rc, sc))
                dve.wait_ge(sall_ok, group + 1)
                F, Fi = k("F%d" % m0, ms), k("Fi%d" % m0, ms)
                link(V.tensor_scalar(Fi.bitcast(I32), k("sall%d" % m0, ms).bitcast(I32), 0x7F800000, None, ALU.bitwise_and))
                link(V.reciprocal(F, Fi))
                link(V.tensor_scalar(F, F, W_TOP, None, ALU.mult))
                link(V.tensor_scalar(Fi, Fi, 1.0 / W_TOP, None, ALU.mult))
                for m in range(ms):
                    last = V.tensor_scalar(sn[:, m * NS:(m + 1) * NS], sc[:, m * NS:(m + 1) * NS],
                                           k("F%d" % (m0 + m)), None, ALU.mult)
                last.then_inc(scales_ok, 1)

            def w_quant(s):
                dve.wait_ge(prep_in, 144 * s + 144)
                V.tensor_tensor(pq, pw, pr, ALU.mult).then_inc(prep_q, 1)
                dve.wait_ge(prep_q, s + 1)
                V.tensor_tensor(pw, pq, ps_, ALU.mult).then_inc(prep_w, 1)

            dve.wait_ge(bias_in, 16)
            for part in range(PARTS):
                V.tensor_copy(bias_part[:, part, :], bias_rest[:, :]).then_inc(bias_step, 1)
                dve.wait_ge(bias_step, 2 * part + 1)
                last = V.tensor_tensor(bias_rest[:, :], bias_rest[:, :], bias_part[:, part, :], ALU.subtract)
                if part < PARTS - 1:
                    last.then_inc(bias_step, 1)
                    dve.wait_ge(bias_step, 2 * part + 2)
            last.then_inc(bias_ok, 1)

            def stats(i, o):
                b, s, r = 4 * i + o, o % 2, o % 4
                dve.wait_ge(in_x[r], 16 * (i + o // 4) + 16)
                def add(t):
                    dve.wait_ge(y_done, 4 * b + t + 1)
                    V.tensor_tensor(xin[r][:, t, :], psum[:, py[t % 2], :], xin[r][:, t, :], ALU.add).then_inc(y_added, 1)

                def bn(t):
                    dve.wait_ge(y_added, 4 * b + t + 1)
                    V.bn_stats(bst[s][:, t, :], xin[r][:, t, :]).then_inc(bn_done, 1)

                add(0)
                add(1)
                bn(0)
                add(2)
                bn(1)
                add(3)
                bn(2)
                bn(3)
                dve.wait_ge(bn_done, 4 * b + 4)
                V.tensor_tensor(mu[s], bst[s][:, :, 1], bst[s][:, :, 4], ALU.add).then_inc(ag_done, 1)
                V.tensor_tensor(n1[s], bst[s][:, :, 1], bst[s][:, :, 4], ALU.subtract).then_inc(ag_done, 1)
                V.tensor_tensor(n2[s], bst[s][:, :, 2], bst[s][:, :, 5], ALU.add).then_inc(ag_done, 1)
                dve.wait_ge(ag_done, 6 * b + 2)
                V.scalar_tensor_tensor(rr[s], n1[s], 0.25, n1[s], ALU.mult, ALU.mult).then_inc(ag_done, 1)
                V.tensor_scalar(mv[s], mu[s], 0.5, None, ALU.mult).then_inc(ag_done, 1)
                dve.wait_ge(ag_done, 6 * b + 4)
                V.scalar_tensor_tensor(rs[s], n2[s], 1.0 / H, rr[s], ALU.mult, ALU.add).then_inc(ag_done, 1)
                dve.wait_ge(ag_done, 6 * b + 6)
                V.tensor_scalar(ve[s], rs[s], LN_EPS, None, ALU.add).then_inc(var_ok, 1)

            def norm(i, o):
                b, s, r = 4 * i + o, o % 2, o % 4
                dve.wait_ge(std_ok, b + 1)
                V.reciprocal(rs[s], sd[s]).then_inc(newton, 1)
                dve.wait_ge(newton, 4 * b + 1)
                V.scalar_tensor_tensor(n1[s], rs[s], -0.5, rs[s], ALU.mult, ALU.mult).then_inc(newton, 1)
                dve.wait_ge(newton, 4 * b + 2)
                V.tensor_tensor(n2[s], n1[s], ve[s], ALU.mult).then_inc(newton, 1)
                dve.wait_ge(newton, 4 * b + 3)
                V.scalar_tensor_tensor(rr[s], n2[s], 1.5, rs[s], ALU.add, ALU.mult).then_inc(newton, 1)
                dve.wait_ge(newton, 4 * b + 4)
                for t in range(ST):
                    last = V.tensor_scalar(xin[r][:, t, :], xin[r][:, t, :], mv[s][:, t:t + 1], rr[s][:, t:t + 1],
                                           ALU.subtract, ALU.mult)
                last.then_inc(yn_ok, 1)

            def reduce_h(i, o):
                b, s = 4 * i + o, o % 2
                dve.wait_ge(h_evac, 4 * b + 4)
                V.tensor_reduce(hmax[:, bass.ds(b, 1)], hT[s], AX.XY, ALU.max,
                                apply_absolute_value=True).then_inc(hmax_ok, 1)

            for b in range(3):
                stats(0, b)
                if b == 2:
                    reduce_h(0, 0)
                norm(0, b)
                block_maxima(0, 0, b)
            scales(0, 0, 1, 3)
            with dve.Fori(0, 3) as i:
                for o in range(3, 7):
                    stats(i, o)
                    reduce_h(i, o - 2)
                    norm(i, o)
                    if o == 4:
                        w_quant(i)
            w_quant(NSL - 1)
            stats(0, B - 1)
            reduce_h(0, B - 3)
            norm(0, B - 1)
            reduce_h(0, B - 2)
            for kt in range(HK):
                dve.wait_ge(h_evac, 4 * (B - 1) + kt + 1)
                V.tensor_reduce(hmax[:, B - 1 + kt:B + kt], hT[1][:, kt, :], AX.X, ALU.max,
                                apply_absolute_value=True).then_inc(hmax_ok, 1)
            dve.wait_ge(hmax_ok, B - 1 + HK)
            V.tensor_reduce(k("hm"), hmax[:, :], AX.X, ALU.max).then_inc(hm_ok, 1)
            dve.wait_ge(hma_ok, 1)
            link(V.tensor_scalar(k("sh"), k("hma"), 1.0 / QA, TINY, ALU.mult, ALU.max))
            link(V.reciprocal(k("rh"), k("sh")))

            def quant_h(j, src=hin):
                if src is hin:
                    dve.wait_ge(hin_in, 16 * j - 16)
                V.tensor_scalar(hq[:, bass.ds(j * TILE, TILE)], src, k("rh"), None, ALU.mult).then_inc(hq_ok, 1)

            def split_h(j, s, mm, hi_done, done):
                wait(dve, mm, 3 * j - 3)
                V.tensor_scalar(a_hi[s], hq[:, bass.ds(j * TILE, TILE)], 1.0, None, ALU.mult).then_inc(hi_done, 1)
                dve.wait_ge(hi_done, j + 1)
                V.tensor_tensor(a_lo[s], hq[:, bass.ds(j * TILE, TILE)], a_hi[s], ALU.subtract).then_inc(done, 1)

            def reduce_gate(n, m, uses):
                dve.wait_ge(g_evac[m % 2], uses + 1)
                V.tensor_reduce(gmax[:, 0, bass.ds(n, 1)], raw[m % 2], AX.X, ALU.max, apply_absolute_value=True)
                V.tensor_reduce(gmax[:, 1, bass.ds(n, 1)], raw[m % 2], AX.X, ALU.max).then_inc(g_red[m % 2], 1)

            for j in range(2):
                quant_h(j, hT[j].rearrange("p k n -> p (k n)"))
                dve.wait_ge(hq_ok, j + 1)
                split_h(j, j, g_mm, hi_ok, split_ok)

            def gate_pair(i, first=False):
                for u in range(2):
                    for c in range(CPB):
                        m = CPB * u + c
                        reduce_gate(6 * i + m, m, 3 * i + m // 2)
                        if first and m < 3:
                            for part in (2 * m, 2 * m + 1):
                                block_maxima(1, part // 3, part % 3)
                        if first and m == 3:
                            scales(1, 1, 2, 9)
                    quant_h(2 * i + u + 2)
                    dve.wait_ge(hq_ok, 2 * i + u + 3)
                    split_h(2 * i + u + 2, u, g_mm, hi_ok, split_ok)
                w_quant(NSL + i)

            gate_pair(0, first=True)
            with dve.Fori(1, B // 2 - 1) as i:
                gate_pair(i)
            for m in range(6):
                reduce_gate(42 + m, m, 21 + m // 2)
                if m == 3:
                    w_quant(3 * NSL - 1)

            for p in range(2):
                dve.wait_ge(g_red[p], NCH // 2)
            V.tensor_reduce(k("gm", 2), gmax[:, :, :], AX.X, ALU.max).then_inc(gm_ok, 1)

            def lower_h(j, s):
                dve.wait_ge(hi2_ok, j + 1)
                V.tensor_tensor(a_lo[s], hq[:, bass.ds(j * TILE, TILE)], a_hi[s], ALU.subtract).then_inc(split2_ok, 1)

            lower_h(0, 0)
            lower_h(1, 1)
            dve.wait_ge(gma_ok, 1)
            link(V.tensor_tensor(k("shg"), k("sh"), k("Fi0"), ALU.mult))
            link(V.tensor_tensor(k("gm"), k("gma"), k("shg"), ALU.mult))
            link(V.tensor_scalar(k("sg"), k("gm"), 1.0 / QA, TINY, ALU.mult, ALU.max))
            link(V.reciprocal(k("rg"), k("sg")))
            link(V.tensor_tensor(k("cq"), k("shg"), k("rg"), ALU.mult))
            link(V.tensor_tensor(flag_sb[:, :], k("gpa"), k("cq"), ALU.mult))
            V.tensor_tensor(k("qf"), flag_sb[:, :], k("sg"), ALU.mult).then_inc(gma_ok, 1)
            dve.wait_ge(fsig_ok, 1)
            link(V.tensor_scalar(k("fu").bitcast(I32), k("fsig"), SIGQ, SIGQ - 1, ALU.mult, ALU.min))
            link(V.scalar_tensor_tensor(k("fpos"), k("qf"), 1.0 / SIGQ, k("fu").bitcast(I32), ALU.mult, ALU.mult))
            V.tensor_scalar(flag_sb[:, :], k("fpos"), NEG_BOUND, None, ALU.is_lt).then_inc(flag_ok, 1)
            link(V.tensor_copy(k("fsel"), k("fpos")))

            def sig_u(n, sdone, udone):
                dve.wait_ge(sdone, n + 1)
                V.tensor_scalar(su16, sig, SIGQ, SIGQ - 1, ALU.mult, ALU.min).then_inc(udone, 1)
                dve.wait_ge(udone, n + 1)

            dve.wait_ge(flag_ok, 1)
            flag = dve.value_load(flag_sb[0:1, 0:1], min_val=0, max_val=1)
            with dve.If(flag > 0):
                def gate_max(n):
                    sig_u(n, f_sig, f_u)
                    wait(dve, f_red, n)
                    V.scalar_tensor_tensor(raw[1], gq, k("sg"), su16, ALU.mult, ALU.mult).then_inc(f_f, 1)
                    dve.wait_ge(f_f, n + 1)
                    V.tensor_reduce(fmax[:, bass.ds(n, 1)], raw[1], AX.X, ALU.max,
                                    apply_absolute_value=True).then_inc(f_red, 1)

                gate_max(0)
                with dve.Fori(1, NCH) as i:
                    gate_max(i)
                dve.wait_ge(f_red, NCH)
                V.tensor_reduce(k("fm"), fmax[:, :], AX.X, ALU.max).then_inc(f_max, 1)
                dve.wait_ge(f_all, 1)
                V.tensor_scalar(k("fsel"), k("fma"), 1.0 / SIGQ, None, ALU.mult).then_inc(f_max, 1)
                dve.wait_ge(f_max, 2)
            link(V.tensor_scalar(k("sf"), k("fsel"), 1.0 / QA, TINY, ALU.mult, ALU.max))
            link(V.reciprocal(k("rf"), k("sf")))
            link(V.tensor_scalar(k("sgn"), k("sg"), 1.0 / SIGQ, None, ALU.mult))
            link(V.tensor_tensor(k("cG"), k("sgn"), k("rf"), ALU.mult))

            def up_chunk(n, m, uses):
                h = m % 2
                sig_u(n, sig_ok, su_ok)
                wait(dve, gg_stored[h], 16 * uses)
                V.scalar_tensor_tensor(gg[h], gq, k("cG"), su16, ALU.mult, ALU.mult).then_inc(gg_ok, 1)
                dve.wait_ge(gg_ok, n + 1)
                dve.wait_ge(up_abs_ok, n + 1)
                V.tensor_reduce(umax[:, bass.ds(n, 1)], raw[h], AX.X, ALU.max, apply_absolute_value=True)
                V.tensor_tensor_reduce(up_abs, gg[h], up_abs, 1.0, 0.0, ALU.mult, ALU.max, gu_max[:, :]).then_inc(u_red[h], 1)
                dve.wait_ge(u_red[h], uses + 1)
                V.tensor_scalar(rmax[:, bass.ds(n, 1)], gu_max[:, :], 1.0, None, ALU.mult).then_inc(u_rmax, 1)

            def up_pair(i):
                for u in range(2):
                    for c in range(CPB):
                        m = CPB * u + c
                        up_chunk(6 * i + m, m, 3 * i + m // 2)
                    lower_h(2 * i + u + 2, u)

            up_pair(0)
            with dve.Fori(1, B // 2 - 1) as i:
                up_pair(i)
            for m in range(6):
                up_chunk(42 + m, m, 21 + m // 2)

            dve.wait_ge(u_rmax, NCH)
            V.tensor_reduce(rmax[:, NCH:NCH + 1], umax[:, :], AX.X, ALU.max).then_inc(um_ok, 1)
            dve.wait_ge(uma_ok, 1)
            link(V.max(top[:, :], rall[:, 0:NCH]))
            V.max_index(top_at[:, :], top[:, :], rall[:, 0:NCH]).then_inc(top_ok, 1)
            dve.wait_ge(top_ok, 1)
            link(V.tensor_tensor(k("shu"), k("sh"), k("Fi1"), ALU.mult))
            link(V.tensor_tensor(k("um"), rall[:, NCH:NCH + 1], k("shu"), ALU.mult))
            link(V.tensor_scalar(k("su"), k("um"), 1.0 / QA, TINY, ALU.mult, ALU.max))
            link(V.reciprocal(k("ru"), k("su")))
            V.tensor_tensor(k("cu"), k("shu"), k("ru"), ALU.mult).then_inc(cu_ok, 1)
            dve.wait_ge(cu_ok, 1)
            link(V.tensor_tensor(k("sfu"), k("sf"), k("su"), ALU.mult))

            link(V.tensor_scalar(k("nb"), k("rf"), NEG_BOUND, 0.5, ALU.mult, ALU.add))
            link(V.scalar_tensor_tensor(k("near"), rall[:, NCH:NCH + 1], k("nb"), top[:, 1:2], ALU.mult, ALU.max))
            link(V.tensor_scalar(k("gap"), k("near"), top[:, 0:1], k("cu"), ALU.subtract, ALU.mult))
            V.tensor_scalar(flag2_sb[:, :], k("gap"), MARGIN, None, ALU.is_ge).then_inc(flag2_ok, 1)
            dve.wait_ge(d_uq, 1)
            V.tensor_tensor_reduce(prod, g_top, u_top, 1.0, 0.0, ALU.mult, ALU.max, omax[:, NCH:NCH + 1]).then_inc(d_prod, 1)
            dve.wait_ge(flag2_ok, 1)
            flag2 = dve.value_load(flag2_sb[0:1, 0:1], min_val=0, max_val=1)
            with dve.If(flag2 > 0):
                def product(n):
                    dve.wait_ge(d_uq, n + 2)
                    V.tensor_tensor(prod, g_top, u_top, ALU.mult).then_inc(d_prod, 1)
                    dve.wait_ge(d_prod, n + 2)
                    V.tensor_reduce(omax[:, bass.ds(n, 1)], prod, AX.X, ALU.max,
                                    apply_absolute_value=True).then_inc(d_red, 1)
                    dve.wait_ge(d_red, n + 1)

                dve.wait_ge(d_prod, 1)
                with dve.Fori(0, NCH) as i:
                    product(i)
                V.tensor_reduce(omax[:, NCH:NCH + 1], omax[:, 0:NCH], AX.X, ALU.max).then_inc(d_red, 1)
                dve.wait_ge(d_red, NCH + 1)
            dve.wait_ge(d_prod, 1)
            V.tensor_copy(k("om"), omax[:, NCH:NCH + 1]).then_inc(om_ok, 1)
            dve.wait_ge(oma_ok, 1)
            link(V.tensor_tensor(k("om"), k("oma"), k("sfu"), ALU.mult))
            link(V.tensor_scalar(k("so"), k("om"), 1.0 / QA, TINY, ALU.mult, ALU.max))
            link(V.reciprocal(k("ro"), k("so")))
            link(V.tensor_tensor(k("cO"), k("sfu"), k("ro"), ALU.mult))
            link(V.tensor_tensor(k("cD"), k("so"), k("Fi2"), ALU.mult))

            def o_chunk(n, p, uses):
                dve.wait_ge(e_uq, n + 1)
                V.scalar_tensor_tensor(oq, gin2[p], k("cO"), uq[p], ALU.mult, ALU.mult).then_inc(e_oq, 1)
                dve.wait_ge(e_oq, n + 1)
                wait(dve, e_mm, n - 1)
                V.tensor_copy(o_hi[p], oq).then_inc(e_hi, 1)
                dve.wait_ge(e_hi, n + 1)
                V.tensor_tensor(o_lo[p], oq, o_hi[p], ALU.subtract).then_inc(e_split, 1)
                dve.wait_ge(e_split, n + 1)

            def residual(j, s, uses):
                dve.wait_ge(e_mm, 3 * j + 3)
                dve.wait_ge(x_in[s], 16 * uses + 16)
                wait(dve, o_stored[s], 16 * uses)
                V.scalar_tensor_tensor(osb[s].rearrange("p t h -> p (t h)"), half1[s], k("cD"),
                                       xres[s].rearrange("p t h -> p (t h)"), ALU.mult, ALU.add).then_inc(res_ok[s], 1)

            o_chunk(0, 0, 0)
            o_chunk(1, 1, 0)
            o_chunk(2, 0, 1)
            o_chunk(3, 1, 1)
            def down_pair(i):
                residual(2 * i, 0, i)
                for n in range(4, 7):
                    o_chunk(6 * i + n, n % 2, 3 * i + n // 2)
                residual(2 * i + 1, 1, i)
                for n in range(7, 10):
                    o_chunk(6 * i + n, n % 2, 3 * i + n // 2)

            down_pair(0)
            with dve.Fori(1, B // 2 - 1) as i:
                down_pair(i)
            residual(B - 2, 0, B // 2 - 1)
            o_chunk(46, 0, 23)
            o_chunk(47, 1, 23)
            dve.wait_ge(x_in[1], 16 * B // 2)
            dve.wait_ge(o_stored[1], 16 * (B // 2 - 1))
            for t in range(ST):
                if t < ST - 1:
                    dve.wait_ge(e_tile, (ST - 1) * (B - 1) + t + 1)
                else:
                    dve.wait_ge(e_mm, NCH)
                V.scalar_tensor_tensor(osb[1][:, t, :], half[1][:, t, :], k("cD"), xres[1][:, t, :],
                                       ALU.mult, ALU.add).then_inc(res_ok[1], 1)

        @block.tensor
        def _(pe):
            T = nc.tensor

            def z_mm(i, o):
                b, s, r = 4 * i + o, o % 2, o % 4
                pe.wait_ge(in_z[r], 32 * (i + o // 4) + 32)
                if not (isinstance(b, int) and b < 2):
                    pe.wait_ge(z_act, b - 1)
                for kt in range(HK):
                    last = T.matmul(psum[:, pz[s], :], wdn[r][:, kt, :], xtin[r][:, kt, :],
                                    start=(kt == 0), stop=(kt == HK - 1))
                last.then_inc(z_done, 1)

            def y_mm(i, o):
                b, s, r = 4 * i + o, o % 2, o % 4
                pe.wait_ge(in_y[r], 32 * (i + o // 4) + 32)
                pe.wait_ge(z_act, b + 1)
                for t in range(ST):
                    if not (isinstance(b, int) and 4 * b + t < 2):
                        pe.wait_ge(y_added, 4 * b + t - 1)
                    T.matmul(psum[:, py[t % 2], :], ones[:, :], bup[r], start=True, stop=False)
                    T.matmul(psum[:, py[t % 2], :], zsb[s][:, t * P:(t + 1) * P], wup[r],
                             start=False, stop=True).then_inc(y_done, 1)

            def transposes(i, o):
                b, r = 4 * i + o, o % 4
                pe.wait_ge(yn_ok, b + 1)
                for kt in range(HK):
                    if not (isinstance(b, int) and b < 1):
                        pe.wait_ge(h_evac, 4 * b + kt - 3)
                    for t in range(ST):
                        last = T.transpose(psum[:, ptr + kt, t * P:(t + 1) * P],
                                           xin[r][:, t, kt * P:(kt + 1) * P], ident[:, :])
                    last.then_inc(tr_done, 1)

            pe.wait_ge(const_ok, 3)
            z_mm(0, 0)
            z_mm(0, 1)
            y_mm(0, 0)
            for b in range(1, 3):
                z_mm(0, b + 1)
                y_mm(0, b)
                transposes(0, b - 1)
            with pe.Fori(0, 3) as i:
                for o in range(3, 7):
                    z_mm(i, o + 1)
                    y_mm(i, o)
                    transposes(i, o - 1)
            y_mm(0, B - 1)
            transposes(0, B - 2)
            transposes(0, B - 1)

            def ffn(matrix, split, evac, done):
                def pair_of_batches(i):
                    for u in range(2):
                        pe.wait_ge(split, 2 * i + u + 1)
                        for c in range(CPB):
                            m = CPB * u + c
                            wait(pe, evac[m % 2], 3 * i + m // 2)
                            for o in range(NB):
                                cs = (c * NB + o) * P
                                for kt in range(HK):
                                    hi = w_hi[:, matrix * NSL + kt, cs:cs + P]
                                    lo = w_lo[:, matrix * NSL + kt, cs:cs + P]
                                    ah, al = a_hi[u][:, kt * S:(kt + 1) * S], a_lo[u][:, kt * S:(kt + 1) * S]
                                    T.matmul(half[m % 2][:, o, :], hi, ah, start=(kt == 0), stop=False)
                                    T.matmul(half[m % 2][:, o, :], hi, al, start=False, stop=False)
                                    last = T.matmul(half[m % 2][:, o, :], lo, ah, start=False, stop=(kt == HK - 1))
                            last.then_inc(done, 1)

                pair_of_batches(0)
                with pe.Fori(1, B // 2) as i:
                    pair_of_batches(i)

            pe.wait_ge(prep_lo, NSL)
            pe.wait_ge(h_evac, 4 * B)
            ffn(0, split_ok, g_evac, g_mm)
            pe.wait_ge(prep_lo, 2 * NSL)
            for p in range(2):
                pe.wait_ge(g_evac[p], NCH // 2)
            ffn(1, split2_ok, u_evac, u_mm)

            pe.wait_ge(prep_lo, 3 * NSL)
            for p in range(2):
                pe.wait_ge(u_evac[p], NCH // 2)
            def down_pair(i):
                for u in range(2):
                    wait(pe, res_ok[u], i)
                    for c in range(CPB):
                        m = CPB * u + c
                        pe.wait_ge(e_split, 6 * i + m + 1)
                        for t in range(ST):
                            for o in range(NB):
                                kt = c * NB + o
                                sl, at = 2 * NSL + kt // 3, (kt % 3) * H
                                hi, lo = w_hi[:, sl, at:at + H], w_lo[:, sl, at:at + H]
                                ts = slice(o * S + t * P, o * S + (t + 1) * P)
                                ah, al = o_hi[m % 2][:, ts], o_lo[m % 2][:, ts]
                                first, end = (c == 0 and o == 0), (c == CPB - 1 and o == NB - 1)
                                T.matmul(half[u][:, t, :], ah, hi, start=first, stop=False)
                                T.matmul(half[u][:, t, :], ah, lo, start=False, stop=False)
                                last = T.matmul(half[u][:, t, :], al, hi, start=False, stop=end)
                            if c == CPB - 1 and t < ST - 1:
                                last.then_inc(e_tile, 1)
                        last.then_inc(e_mm, 1)

            down_pair(0)
            with pe.Fori(1, B // 2) as i:
                down_pair(i)


def kernel(x, itok_B_0_6, L0_cond_down_w, L0_cond_down_b, L0_cond_up_w, L0_cond_up_b, L0_cond_ln_g,
           L0_cond_ln_b, L0_ffn_w_gate, L0_ffn_w_up, L0_ffn_w_down):
    import numpy as np
    import concourse.bacc as bacc
    from concourse.bass_utils import run_bass_kernel_spmd

    profiles = L0_cond_down_w.shape[0]

    def per_partition(v):
        return np.transpose(np.reshape(v, (profiles, HK, P)), (0, 2, 1))

    cols = np.concatenate([per_partition(L0_cond_ln_g), per_partition(L0_cond_ln_b),
                           np.reshape(L0_cond_down_b, (profiles, P, 1))], axis=2)

    def blocks_in(w):
        return np.reshape(np.transpose(np.reshape(w, (I, H // BLK, BLK)), (1, 0, 2)), (P, NS * BLK))

    def blocks_down(w):
        v = np.reshape(w, (H, NSL, 3, 4, BLK))
        return np.reshape(np.transpose(v, (1, 3, 2, 0, 4)), (P, NS * BLK))

    def slices_in(w):
        return np.reshape(np.transpose(w, (1, 0)), (NSL, P, SL))

    def slices_down(w):
        v = np.reshape(np.transpose(w, (1, 0)), (NSL, 3, P, H))
        return np.reshape(np.transpose(v, (0, 2, 1, 3)), (NSL, P, SL))

    arrays = {
        "x_in": x,
        "xT_in": np.transpose(x, (0, 2, 1)),
        "ids_in": np.reshape(itok_B_0_6, (1, B)),
        "down_w": L0_cond_down_w,
        "up_w": L0_cond_up_w,
        "up_b": L0_cond_up_b,
        "cols": cols,
        "w_blocks": np.stack([blocks_in(L0_ffn_w_gate), blocks_in(L0_ffn_w_up), blocks_down(L0_ffn_w_down)]),
        "w_slices": np.concatenate([slices_in(L0_ffn_w_gate), slices_in(L0_ffn_w_up), slices_down(L0_ffn_w_down)]),
    }
    arrays = {n: np.ascontiguousarray(a) for n, a in arrays.items()}
    nc = bacc.Bacc("TRN2", target_bir_lowering=False, num_devices=1)
    aps = [nc.dram_tensor(n, a.shape, mybir.dt.from_np(a.dtype), kind="ExternalInput").ap() for n, a in arrays.items()]
    out = nc.dram_tensor("out", (B, S, H), F32, kind="ExternalOutput").ap()
    adaln_ffn(nc, *aps, out)
    r = run_bass_kernel_spmd(nc, [arrays], core_ids=[0])
    return r.results[0]["out"]
```

```python
import concourse.bass as bass
from concourse import mybir
from contextlib import ExitStack

F32, F16, BF16 = mybir.dt.float32, mybir.dt.float16, mybir.dt.bfloat16
I16, U16, I32, U32 = mybir.dt.int16, mybir.dt.uint16, mybir.dt.int32, mybir.dt.uint32
ALU = mybir.AluOpType
ACT = mybir.ActivationFunctionType
AX = mybir.AxisListType

P = 128
B, S, H = 16, 512, 512
KB = 128
I = 1536
HK = H // P
ST = S // P
TILE = HK * S
NB = 4
CH = NB * S
CPB = I // P // NB
NCH = B * CPB
SL = 1536
NSL = 4
BLK = 32
NS = I * H // BLK // P
LN_EPS = 1e-5
QA = 32767.0
QW = 7.0
TINY = 1e-12
SIGQ = 65536.0
W_TOP = 4096.0
NEG_BOUND = 0.28
PARTS = 3
MARGIN = -36000.0


def adaln_ffn(nc, x, xT, ids, wd_dn, wu_dn, upb, cols, wnat, wtr, out):
    h_scr = nc.dram_tensor("h_scr", (B - 2, P, TILE), F32).ap()
    s_scr = nc.dram_tensor("s_scr", (3, P, NS), F32).ap()
    r_scr = nc.dram_tensor("r_scr", (3, P, NS), F32).ap()
    gate_scr = nc.dram_tensor("gate_scr", (NCH, P, CH), F32).ap()
    up_scr = nc.dram_tensor("up_scr", (NCH, P, CH), F32).ap()
    b_scr = nc.dram_tensor("b_scr", (upb.shape[0], PARTS, H), BF16).ap()
    g_scr = nc.dram_tensor("g_scr", (NCH, P, CH), I16).ap()

    with ExitStack() as ctx:
        def sb(name, shape, dt):
            return ctx.enter_context(nc.sbuf_tensor(name, shape, dt))

        def sem(name):
            return ctx.enter_context(nc.semaphore(name))

        def pair(name):
            return [sem(name + "0"), sem(name + "1")]

        w_hi = sb("w_hi", [P, 3 * NSL, SL], F16)
        w_lo = sb("w_lo", [P, 3 * NSL, SL], F16)
        hq_mem = sb("hq_mem", [P, B * TILE // 2], F32)
        arena = sb("arena", [P, 15872], F32)
        ident = sb("ident", [P, P], F32)
        ones = sb("ones", [PARTS, P], BF16)
        n_prof = upb.shape[0]
        bias_rest = sb("bias_rest", [n_prof, H], F32)
        bias_part = sb("bias_part", [n_prof, PARTS, H], BF16)
        ids_sb = sb("ids_sb", [1, B], I32)
        flag_sb = sb("flag_sb", [P, 1], I32)
        hmax = sb("hmax", [P, B - 1 + HK], F32)
        gmax = sb("gmax", [P, 2, NCH], F32)
        umax = sb("umax", [P, NCH + 1], F32)
        rmax = sb("rmax", [P, NCH + 1], F32)
        rall = sb("rall", [P, NCH + 1], F32)
        top = sb("top", [P, 8], F32)
        top_at = sb("top_at", [P, 8], U32)
        flag2_sb = sb("flag2_sb", [P, 1], I32)
        omax = sb("omax", [P, NCH + 2], F32)
        fmax = sb("fmax", [P, NCH], F32)
        K = sb("K", [P, 64], F32)
        gu_max = sb("gu_max", [P, 2], F32)

        def carve(mem, at, cols_, dt):
            size = 2 if dt in (F16, I16, U16, BF16) else 4
            v = mem[:, at // 4:(at + cols_ * size) // 4]
            return v if dt == F32 else v.bitcast(dt)

        hq = hq_mem[:, :].bitcast(I16)

        def prep_room(at):
            return [carve(arena, at + a, SL, F32) for a in (0, 6144, 12288)] + [carve(arena, at + 18432, SL, I16)]
        prep = prep_room(0)
        prep_g = prep_room(21504)
        def mem3(mem, at, a, b):
            return carve(mem, at, a * b, F32).rearrange("p (a b) -> p a b", a=a)
        wm1 = w_hi[:, NSL:, :].rearrange("p a b -> p (a b)").bitcast(F32)
        wm2 = w_lo[:, NSL:, :].rearrange("p a b -> p (a b)").bitcast(F32)
        R4 = range(4)
        nat = [[carve(arena, 21504 + p * 8192, 2048, F32) for p in range(3)],
               [carve(wm1, p * 8192, 2048, F32) for p in range(3)]]

        def small(mem, at, m):
            return [carve(mem, at + k * m * NS * 4, m * NS, F32) for k in range(5)]
        nat_m, nat_s, nat_t, nat_r, nat_c = zip(small(arena, 46080, 1), small(wm2, 0, 2))
        xin = [mem3(hq_mem, p * 8192, ST, H) for p in R4]
        xtin = [mem3(hq_mem, 32768 + p * 8192, HK, S) for p in R4]
        wdn = [mem3(wm1, p * 2048, HK, KB) for p in R4]
        wup = [carve(wm1, 8192 + p * 2048, H, F32) for p in R4]
        bup = [wm1[0:PARTS, (16384 + p * 1024) // 4:(17408 + p * 1024) // 4].bitcast(BF16) for p in R4]
        zsb = [carve(wm2, p * 2048, S, F32) for p in range(2)]
        hT = [mem3(wm2, 4096 + p * 8192, HK, S) for p in range(2)]
        col = [carve(wm2, 20480 + p * 64, 9, F32) for p in R4]
        bst = [mem3(wm2, 20736 + p * 128, ST, 6) for p in range(2)]
        mu, mv, ve, sd, rs, n1, n2, rr, shift = [[carve(wm2, 20992 + n * 32 + p * 16, ST, F32) for p in range(2)]
                                          for n in range(9)]

        hin = carve(arena, 21504, TILE, F32)
        a_hi = [carve(arena, 29696 + p * 4096, TILE, F16) for p in range(2)]
        a_lo = [carve(arena, 37888 + p * 4096, TILE, F16) for p in range(2)]
        raw = [carve(arena, 46080 + p * 8192, CH, F32) for p in range(2)]
        assert 46080 + 16384 <= 15872 * 4
        gin = [carve(arena, p * 8192, CH, F32) for p in range(2)]
        wg1 = w_hi[:, 0:NSL, :].rearrange("p a b -> p (a b)").bitcast(F32)
        wg2 = w_lo[:, 0:NSL, :].rearrange("p a b -> p (a b)").bitcast(F32)
        su16 = carve(arena, 20480, CH, U16)
        gg = [carve(arena, 24576, CH, I16), carve(wg1, 8192, CH, I16)]
        up_abs = carve(wg1, 0, CH, F32)
        sig = carve(wg2, 0, CH, F32)
        gq = carve(wg2, 8192, CH, I16)

        gin2 = [carve(arena, p * 4096, CH, I16) for p in range(2)]
        pin2 = [carve(arena, 8192 + p * 8192, CH, F32) for p in range(2)]
        uq = [carve(arena, 24576 + p * 4096, CH, I16) for p in range(2)]
        g_top, u_top = [carve(hq_mem, 49152 + p * 4096, CH, I16) for p in range(2)]
        p_top = carve(hq_mem, 57344, CH, F32)
        prod = carve(arena, 32768, CH, F32)
        oq = carve(arena, 40960, CH, I16)
        o_hi = [carve(hq_mem, p * 4096, CH, F16) for p in range(2)]
        o_lo = [carve(hq_mem, 8192 + p * 4096, CH, F16) for p in range(2)]
        xres = [mem3(hq_mem, 16384 + p * 8192, ST, H) for p in range(2)]
        osb = [mem3(hq_mem, 32768 + p * 8192, ST, H) for p in range(2)]

        psum = ctx.enter_context(nc.psum_tensor("psum", [P, 8, 512], F32))
        half = [psum[:, 4 * p:4 * p + 4, :] for p in range(2)]
        half1 = [h.rearrange("p a n -> p (a n)") for h in half]
        halves = [slice(q * CH // 2, (q + 1) * CH // 2) for q in range(2)]
        pz, py, ptr = [0, 1], [2, 3], 4

        names = ("smax0 smax1 smax2 sall0 sall1 sall2 F0 F1 F2 Fi0 Fi1 Fi2 hm hma sh rh "
                 "gm gp gma gpa shg sg rg cq qf fsig fu fpos fm fma fsel sf rf cG sgn um uma shu su ru cu "
                 "om oma sfu so ro cO cD gap nb near").split()

        def k(n, w=1):
            a = names.index(n)
            return K[:, a:a + w]

        ids_in = sem("ids_in")
        const_ok = sem("const_ok")
        kstep = sem("kstep")
        nat_in, nat_red = [sem("nat_in%d" % p) for p in range(3)], sem("nat_red")
        bias_in, bias_step, bias_ok, bias_out = sem("bias_in"), sem("bias_step"), sem("bias_ok"), sem("bias_out")
        smax_ok, sall_ok = sem("smax_ok"), sem("sall_ok")
        scales_ok, scr_out = sem("scales_ok"), sem("scr_out")
        prep_in, prep_g_in, prep_q = sem("prep_in"), sem("prep_g_in"), sem("prep_q")
        prep_w, prep_hi, prep_lo = sem("prep_w"), sem("prep_hi"), sem("prep_lo")
        in_z, in_c, in_y, in_x = [[sem("in_%s%d" % (v, p)) for p in range(4)] for v in "zcyx"]
        z_done, z_act, y_done, y_added = sem("z_done"), sem("z_act"), sem("y_done"), sem("y_added")
        bn_done, ag_done, var_ok, std_ok = sem("bn_done"), sem("ag_done"), sem("var_ok"), sem("std_ok")
        newton, shift_ok, yn_ok, yn_half_ok, tr_done, h_evac = sem("newton"), sem("shift_ok"), sem("yn_ok"), sem("yn_half_ok"), sem("tr_done"), sem("h_evac")
        hmax_ok, h_stored = sem("hmax_ok"), pair("h_stored")
        hm_ok, hma_ok = sem("hm_ok"), sem("hma_ok")
        hin_in, hq_ok, hi_ok, split_ok = sem("hin_in"), sem("hq_ok"), sem("hi_ok"), sem("split_ok")
        g_mm, g_evac, g_red, g_stored = sem("g_mm"), pair("g_evac"), pair("g_red"), pair("g_stored")
        gm_ok, gma_ok, fsig_ok, flag_ok = sem("gm_ok"), sem("gma_ok"), sem("fsig_ok"), sem("flag_ok")
        f_in, f_q, f_sig, f_u, f_f = pair("f_in"), sem("f_q"), sem("f_sig"), sem("f_u"), sem("f_f")
        f_red, f_max, f_all = sem("f_red"), sem("f_max"), sem("f_all")
        hi2_ok, split2_ok = sem("hi2_ok"), sem("split2_ok")
        u_mm, u_half_mm, u_evac, u_red, u_stored = sem("u_mm"), sem("u_half_mm"), pair("u_evac"), pair("u_red"), pair("u_stored")
        gin_in, gq_ok, sig_ok, su_ok = pair("gin_in"), sem("gq_ok"), sem("sig_ok"), sem("su_ok")
        gg_ok, gg_stored = sem("gg_ok"), pair("gg_stored")
        um_ok, uma_ok, top_ok, cu_ok, flag2_ok = sem("um_ok"), sem("uma_ok"), sem("top_ok"), sem("cu_ok"), sem("flag2_ok")
        up_abs_ok, u_rmax = sem("up_abs_ok"), sem("u_rmax")
        top_in, d_in, d_uq, d_prod, d_red = pair("top_in"), sem("d_in"), sem("d_uq"), sem("d_prod"), sem("d_red")
        om_ok, oma_ok = sem("om_ok"), sem("oma_ok")
        e_in, e_uq, e_oq, e_hi, e_split, e_first = pair("e_in"), sem("e_uq"), sem("e_oq"), sem("e_hi"), sem("e_split"), sem("e_first")
        e_mm, e_tile, x_in, res_ok, o_stored = sem("e_mm"), sem("e_tile"), pair("x_in"), pair("res_ok"), pair("o_stored")

        def wait(engine, semaphore, value):
            if not (isinstance(value, int) and value <= 0):
                engine.wait_ge(semaphore, value)

        block = ctx.enter_context(nc.Block())

        @block.sync
        def _(sp):
            sp.dma_start(ids_sb[:, :], ids).then_inc(ids_in, 16)
            sp.dma_start(bias_rest[:, :], upb).then_inc(bias_in, 16)

            def load_blocks(group, m):
                for part in range(3):
                    if m == 2:
                        sp.wait_ge(nat_red, 3 + part + 1)
                    sp.dma_start(nat[group][part], wnat[m, :, part * 2048:(part + 1) * 2048]).then_inc(nat_in[part], 16)

            s_rows = s_scr.rearrange("m p n -> (m p n)").rearrange("(s q c) -> s q c", q=4, c=SL)
            r_rows = r_scr.rearrange("m p n -> (m p n)").rearrange("(s q c) -> s q c", q=4, c=SL)

            def spill_scales(group, ms, done):
                sp.wait_ge(scales_ok, group + 1)
                for n, m in enumerate(ms):
                    for scr, src in ((s_scr, nat_c), (r_scr, nat_r)):
                        sp.dma_start(scr[m], src[group][:, n * NS:(n + 1) * NS]).then_inc(scr_out, 16)
                sp.wait_ge(scr_out, done)

            def load_xT(b, s):
                sp.dma_start(xtin[s], xT[bass.ds(b, 1)].rearrange("a (k p) t -> p (a k) t", p=P)).then_inc(in_z[s], 16)

            def profile(b):
                return sp.value_load(ids_sb[0:1, bass.ds(b, 1)], min_val=0, max_val=n_prof - 1)

            def load_wd(b, s):
                p = profile(b)
                sp.dma_start(wdn[s], wd_dn[bass.ds(p, 1)].rearrange("a (k p) n -> p (a k) n", p=P)).then_inc(in_z[s], 16)

            def load_z(b, s):
                load_xT(b, s)
                load_wd(b, s)

            def load_col(b, s):
                p = profile(b)
                sp.dma_start(col[s], cols[bass.ds(p, 1)].rearrange("a p n -> p (a n)")).then_inc(in_c[s], 16)

            def load_y(b, s, first=False):
                p = profile(b)
                sp.dma_start(wup[s], wu_dn[bass.ds(p, 1)].rearrange("a p n -> p (a n)")).then_inc(in_y[s], 16)
                if first:
                    sp.wait_ge(bias_out, 16)
                sp.dma_start(bup[s], b_scr[bass.ds(p, 1)].rearrange("a r n -> (a r) n")).then_inc(in_y[s], 16)

            def load_x_in(b, s):
                sp.dma_start(xin[s], x[bass.ds(b, 1)].rearrange("a (t p) h -> p (a t) h", p=P)).then_inc(in_x[s], 16)

            def store_h(b, s):
                sp.dma_start(h_scr[bass.ds(b, 1)].rearrange("a p n -> p (a n)"),
                             hT[s].rearrange("p k n -> p (k n)")).then_inc(h_stored[s], 16)

            def step(b, r, x_left=True, yz_left=True):
                sp.wait_ge(h_evac, 4 * b + 4)
                store_h(b, r % 2)
                if x_left:
                    load_col(b + 4, r)
                    load_x_in(b + 4, r)
                if yz_left:
                    load_y(b + 5, (r + 1) % 4)
                    load_z(b + 5, (r + 1) % 4)

            def load_slice(s, room=prep, arrived=prep_in):
                sp.dma_start(room[0], wtr[bass.ds(s, 1)].rearrange("a p n -> p (a n)")).then_inc(arrived, 16)
                for dst, rows in ((room[1], r_rows), (room[2], s_rows)):
                    for q in range(4):
                        src = rows[bass.ds(s, 1), q, :].partition_broadcast(BLK)
                        sp.dma_start(dst[32 * q:32 * q + 32, :], src.rearrange("r a n -> r (a n)")).then_inc(arrived, 16)

            load_xT(0, 0)
            sp.wait_ge(ids_in, 16)
            load_wd(0, 0)
            load_col(0, 0)
            load_z(1, 1)
            sp.wait_ge(bias_ok, 1)
            sp.dma_start(b_scr, bias_part[:, :, :]).then_inc(bias_out, 16)
            load_x_in(0, 0)
            load_y(0, 0, True)
            load_z(2, 2)
            load_col(1, 1)
            load_y(1, 1)
            load_x_in(1, 1)
            load_col(2, 2)
            load_z(3, 3)
            load_x_in(2, 2)
            load_y(2, 2)
            load_blocks(0, 0)
            load_y(3, 3)
            load_col(3, 3)
            load_x_in(3, 3)
            sp.wait_ge(z_act, 1)
            load_z(4, 0)
            sp.wait_ge(y_done, 4)
            load_y(4, 0)
            step(0, 0)
            step(1, 1)
            spill_scales(0, [0], 32)
            step(2, 2)
            load_slice(0)
            with sp.Fori(0, 2) as i:
                step(4 * i + 3, 3)
                step(4 * i + 4, 0)
                step(4 * i + 5, 1)
                step(4 * i + 6, 2)
                sp.wait_ge(prep_lo, i + 1)
                load_slice(i + 1)
            step(11, 3, yz_left=False)
            load_slice(NSL - 1, prep_g, prep_g_in)
            step(12, 0, x_left=False, yz_left=False)
            step(13, 1, x_left=False, yz_left=False)
            sp.wait_ge(y_done, 4 * B)

            sp.wait_ge(h_stored[0], 16 * (B // 2 - 1))
            sp.wait_ge(h_stored[1], 16 * (B // 2 - 1))

            def load_h(j):
                sp.dma_start(hin, h_scr[bass.ds(j - 2, 1)].rearrange("a p n -> p (a n)")).then_inc(hin_in, 16)

            def store_raw(n, m, evac, scr, stored, uses):
                sp.wait_ge(evac[m % 2], uses + 1)
                sp.dma_start(scr[bass.ds(n, 1)].rearrange("a p n -> p (a n)"), raw[m % 2]).then_inc(stored[m % 2], 16)

            def gate_pair(i, first=False, last=False):
                for m in range(6):
                    store_raw(6 * i + m, m, g_evac, gate_scr, g_stored, 3 * i + m // 2)
                    if m % CPB == 0 and not last:
                        j = 2 * i + m // CPB + 2
                        sp.wait_ge(hq_ok, j)
                        load_h(j)
                    if m == 0 and first:
                        load_blocks(1, 2)
                    if m == 3 and first:
                        spill_scales(1, [1, 2], 96)
                        load_slice(NSL)
                    if m == 2 and not first:
                        sp.wait_ge(prep_lo, NSL + i)
                        load_slice(NSL + i)

            load_blocks(1, 1)
            gate_pair(0, first=True)
            with sp.Fori(1, B // 2 - 1) as i:
                gate_pair(i)
            gate_pair(B // 2 - 1, last=True)
            sp.wait_ge(g_stored[0], 16 * NCH // 2)
            sp.wait_ge(g_stored[1], 16 * NCH // 2)
            sp.wait_ge(prep_lo, 3 * NSL)

            def load_gate(n, p, done):
                sp.dma_start(gin[p], gate_scr[bass.ds(n, 1)].rearrange("a p n -> p (a n)")).then_inc(done[p], 16)

            sp.wait_ge(flag_ok, 1)
            flag = sp.value_load(flag_sb[0:1, 0:1], min_val=0, max_val=1)
            with sp.If(flag > 0):
                load_gate(0, 0, f_in)
                load_gate(1, 1, f_in)
                with sp.Fori(1, NCH // 2) as i:
                    for p in range(2):
                        sp.wait_ge(f_q, 2 * i + p - 1)
                        load_gate(2 * i + p, p, f_in)
                sp.wait_ge(f_q, NCH)
            load_gate(0, 0, gin_in)
            load_gate(1, 1, gin_in)

            def up_chunk(n, m, uses, last):
                store_raw(n, m, u_evac, up_scr, u_stored, uses)
                sp.wait_ge(gg_ok, n + 1)
                if not last:
                    load_gate(n + 2, m % 2, gin_in)
                sp.dma_start(g_scr[bass.ds(n, 1)].rearrange("a p n -> p (a n)"), gg[m % 2]).then_inc(gg_stored[m % 2], 16)

            with sp.Fori(0, B // 2 - 1) as i:
                for m in range(6):
                    up_chunk(6 * i + m, m, 3 * i + m // 2, False)
            def load_gu(n, p, done):
                sp.dma_start(gin2[p], g_scr[bass.ds(n, 1)].rearrange("a p n -> p (a n)")).then_inc(done[p], 16)
                sp.dma_start(pin2[p], up_scr[bass.ds(n, 1)].rearrange("a p n -> p (a n)")).then_inc(done[p], 16)

            for m in range(5):
                up_chunk(42 + m, m, 21 + m // 2, m >= 4)
            sp.wait_ge(gq_ok, NCH)
            load_gu(0, 0, e_in)
            sp.wait_ge(gg_ok, NCH)
            sp.dma_start(g_scr[NCH - 1], gg[1]).then_inc(gg_stored[1], 16)
            for q in range(2):
                sp.wait_ge(u_evac[1], NCH // 2 + q)
                sp.dma_start(up_scr[NCH - 1][:, halves[q]], raw[1][:, halves[q]]).then_inc(u_stored[1], 16)
            for p in range(2):
                sp.wait_ge(u_stored[p], 16 * (NCH // 2 + p))
                sp.wait_ge(gg_stored[p], 16 * NCH // 2)

            def load_top(n):
                sp.dma_start(p_top, up_scr[bass.ds(n, 1)].rearrange("a p n -> p (a n)")).then_inc(d_in, 16)
                sp.dma_start(g_top, g_scr[bass.ds(n, 1)].rearrange("a p n -> p (a n)")).then_inc(d_in, 16)

            sp.wait_ge(top_ok, 1)
            at = sp.value_load(top_at[0:1, 0:1], min_val=0, max_val=NCH - 1)
            for q in range(2):
                for dst, scr in ((p_top, up_scr), (g_top, g_scr)):
                    sp.dma_start(dst[:, halves[q]], scr[bass.ds(at, 1), :, halves[q]].rearrange("a p n -> p (a n)")).then_inc(top_in[q], 16)
            load_gu(1, 1, e_in)
            sp.wait_ge(flag2_ok, 1)
            flag2 = sp.value_load(flag2_sb[0:1, 0:1], min_val=0, max_val=1)
            with sp.If(flag2 > 0):
                with sp.Fori(0, NCH) as i:
                    sp.wait_ge(d_prod, i + 2)
                    load_top(i)

            def load_x(batch, s):
                sp.dma_start(xres[s], x[bass.ds(batch, 1)].rearrange("a (t p) h -> p (a t) h", p=P)).then_inc(x_in[s], 16)

            load_x(B - 2, 0)
            load_x(B - 1, 1)
            with sp.Fori(0, B // 2 - 1) as i:
                for m in range(6):
                    sp.wait_ge(e_oq, 6 * i + m + 1)
                    load_gu(6 * i + m + 2, m % 2, e_in)
                    if m == 4:
                        sp.wait_ge(res_ok[0], i + 1)
                        load_x(2 * i, 0)
                sp.wait_ge(res_ok[1], i + 1)
                load_x(2 * i + 1, 1)
            for m in range(4):
                sp.wait_ge(e_oq, 42 + m + 1)
                load_gu(42 + m + 2, m % 2, e_in)
            sp.wait_ge(o_stored[0], 16 * B // 2)
            sp.wait_ge(o_stored[1], 16 * (B // 2 - 1 + ST))

        @block.gpsimd
        def _(pool):
            RMAX = bass.bass_isa.ReduceOp.max
            nc.gpsimd.memset(ident[:, :], 0.0).then_inc(const_ok, 1)
            nc.gpsimd.memset(ones[:, :], 1.0).then_inc(const_ok, 1)
            pool.wait_ge(const_ok, 2)
            nc.gpsimd.affine_select(out=ident[:, :], in_=ident[:, :], compare_op=ALU.not_equal, fill=1.0,
                                    base=0, pattern=[[-1, P]], channel_multiplier=1).then_inc(const_ok, 1)

            def all_max(after, count, src, dst, done):
                pool.wait_ge(after, count)
                nc.gpsimd.partition_all_reduce(dst, src, P, RMAX).then_inc(done, 1)

            def w_lower(s, room=prep):
                pool.wait_ge(prep_hi, s + 1)
                nc.gpsimd.tensor_tensor(w_lo[:, bass.ds(s, 1), :].rearrange("p a n -> p (a n)"), room[0],
                                        w_hi[:, bass.ds(s, 1), :].rearrange("p a n -> p (a n)"),
                                        ALU.subtract).then_inc(prep_lo, 1)

            all_max(smax_ok, 1, k("smax0"), k("sall0"), sall_ok)
            with pool.Fori(0, NSL - 1) as i:
                w_lower(i)
            all_max(hm_ok, 1, k("hm"), k("hma"), hma_ok)
            w_lower(NSL - 1, prep_g)
            all_max(smax_ok, 2, k("smax1", 2), k("sall1", 2), sall_ok)
            with pool.Fori(0, 2 * NSL) as i:
                w_lower(NSL + i)
            all_max(gm_ok, 1, k("gm", 2), k("gma", 2), gma_ok)
            pool.wait_ge(flag_ok, 1)
            flag = pool.value_load(flag_sb[0:1, 0:1], min_val=0, max_val=1)
            with pool.If(flag > 0):
                all_max(f_max, 1, k("fm"), k("fma"), f_all)
            all_max(um_ok, 1, rmax[:, :], rall[:, :], uma_ok)
            all_max(om_ok, 1, k("om"), k("oma"), oma_ok)

        @block.scalar
        def _(act):
            def w_upper(s, room=prep):
                act.wait_ge(prep_w, s + 1)
                nc.scalar.activation(w_hi[:, bass.ds(s, 1), :].rearrange("p a n -> p (a n)"), room[0],
                                     ACT.Copy).then_inc(prep_hi, 1)

            def relu(i, o):
                b, r = 4 * i + o, o % 4
                act.wait_ge(in_c[r], 16 * (i + o // 4) + 16)
                act.wait_ge(z_done, b + 1)
                if not (isinstance(b, int) and b < 2):
                    act.wait_ge(y_done, 4 * b - 4)
                nc.scalar.activation(zsb[r % 2], psum[:, pz[r % 2], :], ACT.Relu, bias=col[r][:, 8:9]).then_inc(z_act, 1)

            def std(i, o):
                act.wait_ge(var_ok, 4 * i + o + 1)
                nc.scalar.activation(sd[o % 2], ve[o % 2], ACT.Sqrt).then_inc(std_ok, 1)

            def norm(i, o, tiles=range(ST)):
                b, s, r = 4 * i + o, o % 2, o % 4
                act.wait_ge(shift_ok, b + 1)
                for t in tiles:
                    last = nc.scalar.activation(xin[r][:, t, :], xin[r][:, t, :], ACT.Identity,
                                                scale=rr[s][:, t:t + 1], bias=shift[s][:, t:t + 1])
                last.then_inc(yn_ok, 1)

            def evac_h(i, o, tiles=range(HK)):
                b, r = 4 * i + o, o % 4
                if not (isinstance(b, int) and b < 2):
                    act.wait_ge(hmax_ok, b - 1)
                    act.wait_ge(h_stored[r % 2], 32 * i + 16 * (o // 2))
                for kt in tiles:
                    act.wait_ge(tr_done, 4 * b + kt + 1)
                    nc.scalar.activation(hT[r % 2][:, kt, :], psum[:, ptr + kt, :], ACT.Identity,
                                         scale=col[r][:, kt:kt + 1], bias=col[r][:, 4 + kt:5 + kt]).then_inc(h_evac, 1)

            relu(0, 0)
            relu(0, 1)
            std(0, 0)
            norm(0, 0)
            for b in range(1, 3):
                relu(0, b + 1)
                evac_h(0, b - 1)
                std(0, b)
                norm(0, b)
            with act.Fori(0, 3) as i:
                for o in range(3, 7):
                    relu(i, o + 1)
                    evac_h(i, o - 1)
                    std(i, o)
                    norm(i, o)
                w_upper(i)
            evac_h(0, B - 2, range(0, 2))
            std(0, B - 1)
            evac_h(0, B - 2, range(2, HK))
            norm(0, B - 1, range(2, ST))
            evac_h(0, B - 1)
            w_upper(NSL - 1, prep_g)

            def evac(n, m, uses, mm, red, stored, done):
                act.wait_ge(mm, n + 1)
                wait(act, red[m % 2], uses)
                wait(act, stored[m % 2], 16 * uses)
                nc.scalar.activation(raw[m % 2], half1[m % 2], ACT.Copy).then_inc(done[m % 2], 1)

            def upper_h(j, s):
                nc.scalar.activation(a_hi[s], hq[:, bass.ds(j * TILE, TILE)], ACT.Copy).then_inc(hi2_ok, 1)

            def gate_pair(i, last=False):
                for m in range(6):
                    evac(6 * i + m, m, 3 * i + m // 2, g_mm, g_red, g_stored, g_evac)
                    if last and m % CPB == 2:
                        upper_h(m // CPB, m // CPB)
                w_upper(NSL + i)

            gate_pair(0)
            with act.Fori(1, B // 2 - 1) as i:
                gate_pair(i)
            gate_pair(B // 2 - 1, last=True)

            act.wait_ge(gma_ok, 2)
            nc.scalar.activation(k("fsig"), k("qf"), ACT.Sigmoid).then_inc(fsig_ok, 1)
            act.wait_ge(flag_ok, 1)
            flag = act.value_load(flag_sb[0:1, 0:1], min_val=0, max_val=1)

            def gate_sigmoid(n, p, uses, arrived, qdone, u_free, g_free, sdone):
                act.wait_ge(arrived[p], 16 * uses + 16)
                wait(act, g_free, n)
                nc.scalar.activation(gq, gin[p], ACT.Identity, scale=k("cq")).then_inc(qdone, 1)
                act.wait_ge(qdone, n + 1)
                wait(act, u_free, n)
                nc.scalar.activation(sig, gq, ACT.Sigmoid, scale=k("sg")).then_inc(sdone, 1)

            with act.If(flag > 0):
                for p in range(2):
                    gate_sigmoid(p, p, 0, f_in, f_q, f_u, f_f, f_sig)
                with act.Fori(1, NCH // 2) as i:
                    for p in range(2):
                        gate_sigmoid(2 * i + p, p, i, f_in, f_q, f_u, f_f, f_sig)
                act.wait_ge(f_max, 1)

            for p in range(2):
                act.wait_ge(g_stored[p], 16 * NCH // 2)
            def up_chunk(n, m, uses):
                gate_sigmoid(n, m % 2, uses, gin_in, gq_ok, su_ok, gg_ok, sig_ok)
                evac(n, m, uses, u_mm, u_red, u_stored, u_evac)
                act.wait_ge(u_evac[m % 2], uses + 1)
                wait(act, u_red[(m + 1) % 2], uses + m % 2)
                nc.scalar.activation(up_abs, raw[m % 2], ACT.Abs).then_inc(up_abs_ok, 1)

            def up_pair(i):
                for m in range(6):
                    up_chunk(6 * i + m, m, 3 * i + m // 2)
                    if m % CPB == 2:
                        upper_h(2 * i + m // CPB + 2, m // CPB)

            up_pair(0)
            with act.Fori(1, B // 2 - 1) as i:
                up_pair(i)
            for m in range(5):
                up_chunk(42 + m, m, 21 + m // 2)
            gate_sigmoid(NCH - 1, 1, NCH // 2 - 1, gin_in, gq_ok, su_ok, gg_ok, sig_ok)
            act.wait_ge(u_red[1], NCH // 2 - 1)
            act.wait_ge(u_stored[1], 16 * (NCH // 2 - 1))
            act.wait_ge(u_red[0], NCH // 2)
            for q, (products, count) in enumerate(((u_half_mm, NCH), (u_mm, NCH))):
                act.wait_ge(products, count)
                nc.scalar.activation(raw[1][:, halves[q]], half1[1][:, halves[q]], ACT.Copy).then_inc(u_evac[1], 1)
                act.wait_ge(u_evac[1], NCH // 2 + q)
                nc.scalar.activation(up_abs[:, halves[q]], raw[1][:, halves[q]], ACT.Abs).then_inc(up_abs_ok, 1)

            def quant_top(n):
                act.wait_ge(d_in, 32 * n + 32)
                nc.scalar.activation(u_top, p_top, ACT.Identity, scale=k("cu")).then_inc(d_uq, 1)

            def quant_up(p, arrived):
                act.wait_ge(e_in[p], arrived)
                nc.scalar.activation(uq[p], pin2[p], ACT.Identity, scale=k("cu")).then_inc(e_uq, 1)

            act.wait_ge(cu_ok, 1)
            act.wait_ge(gg_stored[0], 16 * NCH // 2)
            quant_up(0, 32)
            for q in range(2):
                act.wait_ge(top_in[q], 32)
                nc.scalar.activation(u_top[:, halves[q]], p_top[:, halves[q]], ACT.Abs, scale=k("cu")).then_inc(d_uq, 1)
            quant_up(1, 32)
            act.wait_ge(flag2_ok, 1)
            flag2 = act.value_load(flag2_sb[0:1, 0:1], min_val=0, max_val=1)
            with act.If(flag2 > 0):
                with act.Fori(0, NCH) as i:
                    quant_top(i)

            def store_out(batch, s, uses):
                act.wait_ge(res_ok[s], uses + 1)
                act.dma_start(out[bass.ds(batch, 1)].rearrange("a (t p) h -> p (a t) h", p=P), osb[s]).then_inc(o_stored[s], 16)

            def down_pair(i, batch):
                for m in range(6):
                    act.wait_ge(e_oq, 6 * i + m + 1)
                    quant_up(m % 2, 32 * (3 * i + m // 2) + 64)
                    if m == 3:
                        store_out(batch, 0, i)
                store_out(batch + 1, 1, i)

            down_pair(0, B - 2)
            with act.Fori(1, B // 2 - 1) as i:
                down_pair(i, 2 * i - 2)
            for m in range(4):
                act.wait_ge(e_oq, 42 + m + 1)
                quant_up(m % 2, 32 * (21 + m // 2) + 64)
            store_out(B - 4, 0, B // 2 - 1)
            for t in range(ST):
                act.wait_ge(res_ok[1], B // 2 - 1 + t + 1)
                act.dma_start(out[B - 3, t * P:(t + 1) * P, :], osb[1][:, t, :]).then_inc(o_stored[1], 16)

        @block.vector
        def _(dve):
            count = [0]

            def link(ins):
                count[0] += 1
                ins.then_inc(kstep, 1)
                dve.wait_ge(kstep, count[0])

            V = nc.vector
            def block_maxima(group, m, part):
                dve.wait_ge(nat_in[part], 16 * (group + m) + 16)
                V.tensor_reduce(nat_m[group][:, m * NS + part * 64:m * NS + (part + 1) * 64],
                                nat[group][part].rearrange("p (b e) -> p b e", e=BLK), AX.X, ALU.max,
                                apply_absolute_value=True).then_inc(nat_red, 1)

            def scales(group, m0, ms, reduced):
                mx, sc, tm, rc, sn = [a[group] for a in (nat_m, nat_s, nat_t, nat_r, nat_c)]
                dve.wait_ge(nat_red, reduced)
                link(V.tensor_scalar(sc, mx, 1.0 / QW, None, ALU.mult))
                link(V.scalar_tensor_tensor(tm, sc, -(QW + 1), mx, ALU.mult, ALU.add))
                link(V.tensor_tensor(tm, tm, sc, ALU.add))
                link(V.scalar_tensor_tensor(tm, tm, 1.0 / QW, sc, ALU.mult, ALU.add))
                link(V.tensor_scalar(sc, tm, TINY, None, ALU.max))
                V.tensor_reduce(k("smax%d" % m0, ms), sc.rearrange("p (m n) -> p m n", m=ms), AX.X, ALU.max).then_inc(smax_ok, 1)
                link(V.reciprocal(rc, sc))
                dve.wait_ge(sall_ok, group + 1)
                F, Fi = k("F%d" % m0, ms), k("Fi%d" % m0, ms)
                link(V.tensor_scalar(Fi.bitcast(I32), k("sall%d" % m0, ms).bitcast(I32), 0x7F800000, None, ALU.bitwise_and))
                link(V.reciprocal(F, Fi))
                link(V.tensor_scalar(F, F, W_TOP, None, ALU.mult))
                link(V.tensor_scalar(Fi, Fi, 1.0 / W_TOP, None, ALU.mult))
                for m in range(ms):
                    last = V.tensor_scalar(sn[:, m * NS:(m + 1) * NS], sc[:, m * NS:(m + 1) * NS],
                                           k("F%d" % (m0 + m)), None, ALU.mult)
                last.then_inc(scales_ok, 1)

            def w_integers(s, n):
                pw, pr, _, pq = prep
                dve.wait_ge(prep_in, 144 * n + 144)
                V.tensor_tensor(pq, pw, pr, ALU.mult).then_inc(prep_q, 1)

            def w_values(s):
                pw, _, ps_, pq = prep
                dve.wait_ge(prep_q, s + 1)
                V.tensor_tensor(pw, pq, ps_, ALU.mult).then_inc(prep_w, 1)

            def w_quant(s):
                w_integers(s, s - 1)
                w_values(s)

            dve.wait_ge(bias_in, 16)
            for part in range(PARTS):
                V.tensor_copy(bias_part[:, part, :], bias_rest[:, :]).then_inc(bias_step, 1)
                dve.wait_ge(bias_step, 2 * part + 1)
                last = V.tensor_tensor(bias_rest[:, :], bias_rest[:, :], bias_part[:, part, :], ALU.subtract)
                if part < PARTS - 1:
                    last.then_inc(bias_step, 1)
                    dve.wait_ge(bias_step, 2 * part + 2)
            last.then_inc(bias_ok, 1)

            def stats(i, o):
                b, s, r = 4 * i + o, o % 2, o % 4
                dve.wait_ge(in_x[r], 16 * (i + o // 4) + 16)
                def add(t):
                    dve.wait_ge(y_done, 4 * b + t + 1)
                    V.tensor_tensor(xin[r][:, t, :], psum[:, py[t % 2], :], xin[r][:, t, :], ALU.add).then_inc(y_added, 1)

                def bn(t):
                    dve.wait_ge(y_added, 4 * b + t + 1)
                    V.bn_stats(bst[s][:, t, :], xin[r][:, t, :]).then_inc(bn_done, 1)

                add(0)
                add(1)
                bn(0)
                add(2)
                bn(1)
                add(3)
                bn(2)
                bn(3)
                dve.wait_ge(bn_done, 4 * b + 4)
                V.tensor_tensor(mu[s], bst[s][:, :, 1], bst[s][:, :, 4], ALU.add).then_inc(ag_done, 1)
                V.tensor_tensor(n1[s], bst[s][:, :, 1], bst[s][:, :, 4], ALU.subtract).then_inc(ag_done, 1)
                V.tensor_tensor(n2[s], bst[s][:, :, 2], bst[s][:, :, 5], ALU.add).then_inc(ag_done, 1)
                dve.wait_ge(ag_done, 6 * b + 2)
                V.scalar_tensor_tensor(rr[s], n1[s], 0.25, n1[s], ALU.mult, ALU.mult).then_inc(ag_done, 1)
                V.tensor_scalar(mv[s], mu[s], 0.5, None, ALU.mult).then_inc(ag_done, 1)
                dve.wait_ge(ag_done, 6 * b + 4)
                V.scalar_tensor_tensor(rs[s], n2[s], 1.0 / H, rr[s], ALU.mult, ALU.add).then_inc(ag_done, 1)
                dve.wait_ge(ag_done, 6 * b + 6)
                V.tensor_scalar(ve[s], rs[s], LN_EPS, None, ALU.add).then_inc(var_ok, 1)

            def factors(i, o):
                b, s, r = 4 * i + o, o % 2, o % 4
                dve.wait_ge(std_ok, b + 1)
                V.reciprocal(rs[s], sd[s]).then_inc(newton, 1)
                dve.wait_ge(newton, 4 * b + 1)
                V.scalar_tensor_tensor(n1[s], rs[s], -0.5, rs[s], ALU.mult, ALU.mult).then_inc(newton, 1)
                dve.wait_ge(newton, 4 * b + 2)
                V.tensor_tensor(n2[s], n1[s], ve[s], ALU.mult).then_inc(newton, 1)
                dve.wait_ge(newton, 4 * b + 3)
                V.scalar_tensor_tensor(rr[s], n2[s], 1.5, rs[s], ALU.add, ALU.mult).then_inc(newton, 1)
                dve.wait_ge(newton, 4 * b + 4)
                V.scalar_tensor_tensor(shift[s], mv[s], -1.0, rr[s], ALU.mult, ALU.mult).then_inc(shift_ok, 1)

            def reduce_h(i, o):
                b, s = 4 * i + o, o % 2
                dve.wait_ge(h_evac, 4 * b + 4)
                V.tensor_reduce(hmax[:, bass.ds(b, 1)], hT[s], AX.XY, ALU.max,
                                apply_absolute_value=True).then_inc(hmax_ok, 1)

            for b in range(3):
                stats(0, b)
                if b == 2:
                    reduce_h(0, 0)
                factors(0, b)
                for part in ((), (0,), (1, 2))[b]:
                    block_maxima(0, 0, part)
            scales(0, 0, 1, 3)
            with dve.Fori(0, 3) as i:
                for o in range(3, 7):
                    stats(i, o)
                    reduce_h(i, o - 2)
                    factors(i, o)
                    if o == 5:
                        w_integers(i, i)
                    if o == 6:
                        w_values(i)
            pw, pr, ps_, pq = prep_g
            dve.wait_ge(prep_g_in, 144)
            V.tensor_tensor(pq, pw, pr, ALU.mult).then_inc(prep_q, 1)
            stats(0, B - 1)
            factors(0, B - 1)
            dve.wait_ge(shift_ok, B)
            last, r = (B - 1) % 2, (B - 1) % 4
            for t in range(2):
                half_norm = V.tensor_scalar(xin[r][:, t, :], xin[r][:, t, :], rr[last][:, t:t + 1],
                                            shift[last][:, t:t + 1], ALU.mult, ALU.add)
            half_norm.then_inc(yn_half_ok, 1)
            reduce_h(0, B - 3)
            dve.wait_ge(prep_q, NSL)
            V.tensor_tensor(pw, pq, ps_, ALU.mult).then_inc(prep_w, 1)
            reduce_h(0, B - 2)
            for kt in range(HK):
                dve.wait_ge(h_evac, 4 * (B - 1) + kt + 1)
                V.tensor_reduce(hmax[:, B - 1 + kt:B + kt], hT[1][:, kt, :], AX.X, ALU.max,
                                apply_absolute_value=True).then_inc(hmax_ok, 1)
            dve.wait_ge(hmax_ok, B - 1 + HK)
            V.tensor_reduce(k("hm"), hmax[:, :], AX.X, ALU.max).then_inc(hm_ok, 1)
            dve.wait_ge(hma_ok, 1)
            link(V.tensor_scalar(k("sh"), k("hma"), 1.0 / QA, TINY, ALU.mult, ALU.max))
            link(V.reciprocal(k("rh"), k("sh")))

            def quant_h(j, src=hin):
                if src is hin:
                    dve.wait_ge(hin_in, 16 * j - 16)
                V.tensor_scalar(hq[:, bass.ds(j * TILE, TILE)], src, k("rh"), None, ALU.mult).then_inc(hq_ok, 1)

            def split_h(j, s, mm, hi_done, done):
                wait(dve, mm, 3 * j - 3)
                V.tensor_scalar(a_hi[s], hq[:, bass.ds(j * TILE, TILE)], 1.0, None, ALU.mult).then_inc(hi_done, 1)
                dve.wait_ge(hi_done, j + 1)
                V.tensor_tensor(a_lo[s], hq[:, bass.ds(j * TILE, TILE)], a_hi[s], ALU.subtract).then_inc(done, 1)

            def reduce_gate(n, m, uses):
                dve.wait_ge(g_evac[m % 2], uses + 1)
                V.tensor_reduce(gmax[:, 0, bass.ds(n, 1)], raw[m % 2], AX.X, ALU.max, apply_absolute_value=True)
                V.tensor_reduce(gmax[:, 1, bass.ds(n, 1)], raw[m % 2], AX.X, ALU.max).then_inc(g_red[m % 2], 1)

            for j in range(2):
                quant_h(j, hT[j].rearrange("p k n -> p (k n)"))
                dve.wait_ge(hq_ok, j + 1)
                split_h(j, j, g_mm, hi_ok, split_ok)

            def lower_h(j, s):
                dve.wait_ge(hi2_ok, j + 1)
                V.tensor_tensor(a_lo[s], hq[:, bass.ds(j * TILE, TILE)], a_hi[s], ALU.subtract).then_inc(split2_ok, 1)

            def gate_pair(i, first=False):
                for u in range(2):
                    for c in range(CPB):
                        m = CPB * u + c
                        reduce_gate(6 * i + m, m, 3 * i + m // 2)
                        if first and m < 3:
                            for part in (2 * m, 2 * m + 1):
                                block_maxima(1, part // 3, part % 3)
                        if first and m == 3:
                            scales(1, 1, 2, 9)
                    quant_h(2 * i + u + 2)
                    dve.wait_ge(hq_ok, 2 * i + u + 3)
                    split_h(2 * i + u + 2, u, g_mm, hi_ok, split_ok)
                w_quant(NSL + i)

            gate_pair(0, first=True)
            with dve.Fori(1, B // 2 - 1) as i:
                gate_pair(i)
            for m in range(6):
                reduce_gate(42 + m, m, 21 + m // 2)
                if m == 3:
                    lower_h(0, 0)
                    w_quant(3 * NSL - 1)

            for p in range(2):
                dve.wait_ge(g_red[p], NCH // 2)
            V.tensor_reduce(k("gm", 2), gmax[:, :, :], AX.X, ALU.max).then_inc(gm_ok, 1)

            lower_h(1, 1)
            dve.wait_ge(gma_ok, 1)
            link(V.tensor_tensor(k("shg"), k("sh"), k("Fi0"), ALU.mult))
            link(V.tensor_tensor(k("gm"), k("gma"), k("shg"), ALU.mult))
            link(V.tensor_scalar(k("sg"), k("gm"), 1.0 / QA, TINY, ALU.mult, ALU.max))
            link(V.reciprocal(k("rg"), k("sg")))
            link(V.tensor_tensor(k("cq"), k("shg"), k("rg"), ALU.mult))
            link(V.tensor_tensor(flag_sb[:, :], k("gpa"), k("cq"), ALU.mult))
            V.tensor_tensor(k("qf"), flag_sb[:, :], k("sg"), ALU.mult).then_inc(gma_ok, 1)
            dve.wait_ge(fsig_ok, 1)
            link(V.tensor_scalar(k("fu").bitcast(I32), k("fsig"), SIGQ, SIGQ - 1, ALU.mult, ALU.min))
            link(V.scalar_tensor_tensor(k("fpos"), k("qf"), 1.0 / SIGQ, k("fu").bitcast(I32), ALU.mult, ALU.mult))
            V.tensor_scalar(flag_sb[:, :], k("fpos"), NEG_BOUND, None, ALU.is_lt).then_inc(flag_ok, 1)
            link(V.tensor_copy(k("fsel"), k("fpos")))

            def sig_u(n, sdone, udone):
                dve.wait_ge(sdone, n + 1)
                V.tensor_scalar(su16, sig, SIGQ, SIGQ - 1, ALU.mult, ALU.min).then_inc(udone, 1)
                dve.wait_ge(udone, n + 1)

            dve.wait_ge(flag_ok, 1)
            flag = dve.value_load(flag_sb[0:1, 0:1], min_val=0, max_val=1)
            with dve.If(flag > 0):
                def gate_max(n):
                    sig_u(n, f_sig, f_u)
                    wait(dve, f_red, n)
                    V.scalar_tensor_tensor(raw[1], gq, k("sg"), su16, ALU.mult, ALU.mult).then_inc(f_f, 1)
                    dve.wait_ge(f_f, n + 1)
                    V.tensor_reduce(fmax[:, bass.ds(n, 1)], raw[1], AX.X, ALU.max,
                                    apply_absolute_value=True).then_inc(f_red, 1)

                gate_max(0)
                with dve.Fori(1, NCH) as i:
                    gate_max(i)
                dve.wait_ge(f_red, NCH)
                V.tensor_reduce(k("fm"), fmax[:, :], AX.X, ALU.max).then_inc(f_max, 1)
                dve.wait_ge(f_all, 1)
                V.tensor_scalar(k("fsel"), k("fma"), 1.0 / SIGQ, None, ALU.mult).then_inc(f_max, 1)
                dve.wait_ge(f_max, 2)
            link(V.tensor_scalar(k("sf"), k("fsel"), 1.0 / QA, TINY, ALU.mult, ALU.max))
            link(V.reciprocal(k("rf"), k("sf")))
            link(V.tensor_scalar(k("sgn"), k("sg"), 1.0 / SIGQ, None, ALU.mult))
            link(V.tensor_tensor(k("cG"), k("sgn"), k("rf"), ALU.mult))

            def up_chunk(n, m, uses):
                h = m % 2
                sig_u(n, sig_ok, su_ok)
                wait(dve, gg_stored[h], 16 * uses)
                V.scalar_tensor_tensor(gg[h], gq, k("cG"), su16, ALU.mult, ALU.mult).then_inc(gg_ok, 1)
                dve.wait_ge(gg_ok, n + 1)
                if isinstance(n, int):
                    dve.wait_ge(u_evac[h], uses + 1)
                else:
                    dve.wait_ge(up_abs_ok, n + 1)
                V.tensor_reduce(umax[:, bass.ds(n, 1)], raw[h], AX.X, ALU.max, apply_absolute_value=True)
                if isinstance(n, int):
                    dve.wait_ge(up_abs_ok, n + 1)
                V.tensor_tensor_reduce(up_abs, gg[h], up_abs, 1.0, 0.0, ALU.mult, ALU.max, gu_max[:, 0:1]).then_inc(u_red[h], 1)
                dve.wait_ge(u_red[h], uses + 1)
                V.tensor_scalar(rmax[:, bass.ds(n, 1)], gu_max[:, 0:1], 1.0, None, ALU.mult).then_inc(u_rmax, 1)

            def up_pair(i):
                for u in range(2):
                    for c in range(CPB):
                        m = CPB * u + c
                        up_chunk(6 * i + m, m, 3 * i + m // 2)
                    lower_h(2 * i + u + 2, u)

            up_pair(0)
            with dve.Fori(1, B // 2 - 1) as i:
                up_pair(i)
            for m in range(5):
                up_chunk(42 + m, m, 21 + m // 2)
            sig_u(NCH - 1, sig_ok, su_ok)
            dve.wait_ge(gg_stored[1], 16 * (NCH // 2 - 1))
            V.scalar_tensor_tensor(gg[1], gq, k("cG"), su16, ALU.mult, ALU.mult).then_inc(gg_ok, 1)
            dve.wait_ge(gg_ok, NCH)
            dve.wait_ge(u_rmax, NCH - 1)
            for q in range(2):
                dve.wait_ge(u_evac[1], NCH // 2 + q)
                V.tensor_reduce(umax[:, NCH - 1 + q:NCH + q], raw[1][:, halves[q]], AX.X, ALU.max,
                                apply_absolute_value=True)
                dve.wait_ge(up_abs_ok, NCH + q)
                V.tensor_tensor_reduce(up_abs[:, halves[q]], gg[1][:, halves[q]], up_abs[:, halves[q]], 1.0, 0.0,
                                       ALU.mult, ALU.max, gu_max[:, q:q + 1]).then_inc(u_red[1], 1)
            dve.wait_ge(u_red[1], NCH // 2 + 1)
            V.tensor_tensor(rmax[:, NCH - 1:NCH], gu_max[:, 0:1], gu_max[:, 1:2], ALU.max).then_inc(u_rmax, 1)

            dve.wait_ge(u_rmax, NCH)
            V.tensor_reduce(rmax[:, NCH:NCH + 1], umax[:, :], AX.X, ALU.max).then_inc(um_ok, 1)
            dve.wait_ge(uma_ok, 1)
            link(V.max(top[:, :], rall[:, 0:NCH]))
            V.max_index(top_at[:, :], top[:, :], rall[:, 0:NCH]).then_inc(top_ok, 1)
            dve.wait_ge(top_ok, 1)
            link(V.tensor_tensor(k("shu"), k("sh"), k("Fi1"), ALU.mult))
            link(V.tensor_tensor(k("um"), rall[:, NCH:NCH + 1], k("shu"), ALU.mult))
            link(V.tensor_scalar(k("su"), k("um"), 1.0 / QA, TINY, ALU.mult, ALU.max))
            link(V.reciprocal(k("ru"), k("su")))
            V.tensor_tensor(k("cu"), k("shu"), k("ru"), ALU.mult).then_inc(cu_ok, 1)
            dve.wait_ge(cu_ok, 1)
            link(V.tensor_tensor(k("sfu"), k("sf"), k("su"), ALU.mult))

            link(V.tensor_scalar(k("nb"), k("rf"), NEG_BOUND, 0.5, ALU.mult, ALU.add))
            link(V.scalar_tensor_tensor(k("near"), rall[:, NCH:NCH + 1], k("nb"), top[:, 1:2], ALU.mult, ALU.max))
            link(V.tensor_scalar(k("gap"), k("near"), top[:, 0:1], k("cu"), ALU.subtract, ALU.mult))
            V.tensor_scalar(flag2_sb[:, :], k("gap"), MARGIN, None, ALU.is_ge).then_inc(flag2_ok, 1)
            for q in range(2):
                dve.wait_ge(d_uq, q + 1)
                V.tensor_tensor_reduce(prod[:, halves[q]], g_top[:, halves[q]], u_top[:, halves[q]], 1.0, 0.0,
                                       ALU.mult, ALU.max, omax[:, NCH + q:NCH + q + 1]).then_inc(d_prod, 1)
            dve.wait_ge(flag2_ok, 1)
            flag2 = dve.value_load(flag2_sb[0:1, 0:1], min_val=0, max_val=1)
            with dve.If(flag2 > 0):
                def product(n):
                    dve.wait_ge(d_uq, n + 3)
                    V.tensor_tensor(prod, g_top, u_top, ALU.mult).then_inc(d_prod, 1)
                    dve.wait_ge(d_prod, n + 3)
                    V.tensor_reduce(omax[:, bass.ds(n, 1)], prod, AX.X, ALU.max,
                                    apply_absolute_value=True).then_inc(d_red, 1)
                    dve.wait_ge(d_red, n + 1)

                dve.wait_ge(d_prod, 2)
                with dve.Fori(0, NCH) as i:
                    product(i)
                V.tensor_reduce(omax[:, NCH:NCH + 1], omax[:, 0:NCH], AX.X, ALU.max).then_inc(d_red, 1)
                dve.wait_ge(d_red, NCH + 1)
            dve.wait_ge(d_prod, 2)
            V.tensor_tensor(k("om"), omax[:, NCH:NCH + 1], omax[:, NCH + 1:NCH + 2], ALU.max).then_inc(om_ok, 1)
            dve.wait_ge(oma_ok, 1)
            link(V.tensor_tensor(k("om"), k("oma"), k("sfu"), ALU.mult))
            link(V.tensor_scalar(k("so"), k("om"), 1.0 / QA, TINY, ALU.mult, ALU.max))
            link(V.reciprocal(k("ro"), k("so")))
            link(V.tensor_tensor(k("cO"), k("sfu"), k("ro"), ALU.mult))
            link(V.tensor_tensor(k("cD"), k("so"), k("Fi2"), ALU.mult))

            def o_chunk(n, p, uses):
                dve.wait_ge(e_uq, n + 1)
                V.scalar_tensor_tensor(oq, gin2[p], k("cO"), uq[p], ALU.mult, ALU.mult).then_inc(e_oq, 1)
                dve.wait_ge(e_oq, n + 1)
                wait(dve, e_mm, n - 1)
                V.tensor_copy(o_hi[p], oq).then_inc(e_hi, 1)
                dve.wait_ge(e_hi, n + 1)
                V.tensor_tensor(o_lo[p], oq, o_hi[p], ALU.subtract).then_inc(e_split, 1)
                dve.wait_ge(e_split, n + 1)

            def residual(j, s, uses):
                dve.wait_ge(e_mm, 3 * j + 3)
                dve.wait_ge(x_in[s], 16 * uses + 16)
                wait(dve, o_stored[s], 16 * uses)
                V.scalar_tensor_tensor(osb[s].rearrange("p t h -> p (t h)"), half1[s], k("cD"),
                                       xres[s].rearrange("p t h -> p (t h)"), ALU.mult, ALU.add).then_inc(res_ok[s], 1)

            dve.wait_ge(e_uq, 1)
            for q, (oq_done, hi_done, split_done) in enumerate(((e_first, e_first, e_first), (e_oq, e_hi, e_split))):
                v = halves[q]
                V.scalar_tensor_tensor(oq[:, v], gin2[0][:, v], k("cO"), uq[0][:, v], ALU.mult, ALU.mult).then_inc(oq_done, 1)
                dve.wait_ge(oq_done, 1)
                V.tensor_copy(o_hi[0][:, v], oq[:, v]).then_inc(hi_done, 1)
                dve.wait_ge(hi_done, 2 if q == 0 else 1)
                V.tensor_tensor(o_lo[0][:, v], oq[:, v], o_hi[0][:, v], ALU.subtract).then_inc(split_done, 1)
            dve.wait_ge(e_split, 1)
            o_chunk(1, 1, 0)
            o_chunk(2, 0, 1)
            o_chunk(3, 1, 1)
            def down_pair(i):
                residual(2 * i, 0, i)
                for n in range(4, 7):
                    o_chunk(6 * i + n, n % 2, 3 * i + n // 2)
                residual(2 * i + 1, 1, i)
                for n in range(7, 10):
                    o_chunk(6 * i + n, n % 2, 3 * i + n // 2)

            down_pair(0)
            with dve.Fori(1, B // 2 - 1) as i:
                down_pair(i)
            residual(B - 2, 0, B // 2 - 1)
            o_chunk(46, 0, 23)
            o_chunk(47, 1, 23)
            dve.wait_ge(x_in[1], 16 * B // 2)
            dve.wait_ge(o_stored[1], 16 * (B // 2 - 1))
            for t in range(ST):
                if t < ST - 1:
                    dve.wait_ge(e_tile, (ST - 1) * (B - 1) + t + 1)
                else:
                    dve.wait_ge(e_mm, NCH)
                V.scalar_tensor_tensor(osb[1][:, t, :], half[1][:, t, :], k("cD"), xres[1][:, t, :],
                                       ALU.mult, ALU.add).then_inc(res_ok[1], 1)

        @block.tensor
        def _(pe):
            T = nc.tensor

            def z_mm(i, o):
                b, s, r = 4 * i + o, o % 2, o % 4
                pe.wait_ge(in_z[r], 32 * (i + o // 4) + 32)
                if not (isinstance(b, int) and b < 2):
                    pe.wait_ge(z_act, b - 1)
                for kt in range(HK):
                    last = T.matmul(psum[:, pz[s], :], wdn[r][:, kt, :], xtin[r][:, kt, :],
                                    start=(kt == 0), stop=(kt == HK - 1))
                last.then_inc(z_done, 1)

            def y_mm(i, o):
                b, s, r = 4 * i + o, o % 2, o % 4
                pe.wait_ge(in_y[r], 32 * (i + o // 4) + 32)
                pe.wait_ge(z_act, b + 1)
                for t in range(ST):
                    if not (isinstance(b, int) and 4 * b + t < 2):
                        pe.wait_ge(y_added, 4 * b + t - 1)
                    T.matmul(psum[:, py[t % 2], :], ones[:, :], bup[r], start=True, stop=False)
                    T.matmul(psum[:, py[t % 2], :], zsb[s][:, t * P:(t + 1) * P], wup[r],
                             start=False, stop=True).then_inc(y_done, 1)

            def transposes(i, o):
                b, r = 4 * i + o, o % 4
                pe.wait_ge(yn_ok, b + 1)
                for kt in range(HK):
                    if not (isinstance(b, int) and b < 1):
                        pe.wait_ge(h_evac, 4 * b + kt - 3)
                    for t in range(ST):
                        last = T.transpose(psum[:, ptr + kt, t * P:(t + 1) * P],
                                           xin[r][:, t, kt * P:(kt + 1) * P], ident[:, :])
                    last.then_inc(tr_done, 1)

            pe.wait_ge(const_ok, 3)
            z_mm(0, 0)
            z_mm(0, 1)
            y_mm(0, 0)
            for b in range(1, 3):
                z_mm(0, b + 1)
                y_mm(0, b)
                transposes(0, b - 1)
            with pe.Fori(0, 3) as i:
                for o in range(3, 7):
                    z_mm(i, o + 1)
                    y_mm(i, o)
                    transposes(i, o - 1)
            y_mm(0, B - 1)
            transposes(0, B - 2)
            pe.wait_ge(yn_half_ok, 1)
            transposes(0, B - 1)

            def ffn(matrix, split, evac, done, earlier=None, half_done=None):
                def pair_of_batches(i):
                    for u in range(2):
                        pe.wait_ge(split, 2 * i + u + 1)
                        for c in range(CPB):
                            m = CPB * u + c
                            wait(pe, evac[m % 2], 3 * i + m // 2)
                            if earlier and isinstance(i, int) and m < 2:
                                pe.wait_ge(earlier[m], NCH // 2)
                            for o in range(NB):
                                cs = (c * NB + o) * P
                                for kt in range(HK):
                                    hi = w_hi[:, matrix * NSL + kt, cs:cs + P]
                                    lo = w_lo[:, matrix * NSL + kt, cs:cs + P]
                                    ah, al = a_hi[u][:, kt * S:(kt + 1) * S], a_lo[u][:, kt * S:(kt + 1) * S]
                                    T.matmul(half[m % 2][:, o, :], hi, ah, start=(kt == 0), stop=False)
                                    T.matmul(half[m % 2][:, o, :], hi, al, start=False, stop=False)
                                    last = T.matmul(half[m % 2][:, o, :], lo, ah, start=False, stop=(kt == HK - 1))
                                if half_done and o == NB // 2 - 1:
                                    last.then_inc(half_done, 1)
                            last.then_inc(done, 1)

                pair_of_batches(0)
                with pe.Fori(1, B // 2) as i:
                    pair_of_batches(i)

            pe.wait_ge(prep_lo, NSL)
            pe.wait_ge(h_evac, 4 * B)
            ffn(0, split_ok, g_evac, g_mm)
            pe.wait_ge(prep_lo, 2 * NSL)
            ffn(1, split2_ok, u_evac, u_mm, g_evac, u_half_mm)

            pe.wait_ge(prep_lo, 3 * NSL)
            for p in range(2):
                pe.wait_ge(u_evac[p], NCH // 2 + p)
            def first_chunk():
                for q, (ready, count) in enumerate(((e_first, 3), (e_split, 1))):
                    pe.wait_ge(ready, count)
                    for t in range(ST):
                        for kt in range(q * NB // 2, (q + 1) * NB // 2):
                            sl, at = 2 * NSL + kt // 3, (kt % 3) * H
                            hi, lo = w_hi[:, sl, at:at + H], w_lo[:, sl, at:at + H]
                            ts = slice(kt * S + t * P, kt * S + (t + 1) * P)
                            ah, al = o_hi[0][:, ts], o_lo[0][:, ts]
                            T.matmul(half[0][:, t, :], ah, hi, start=(kt == 0), stop=False)
                            T.matmul(half[0][:, t, :], ah, lo, start=False, stop=False)
                            last = T.matmul(half[0][:, t, :], al, hi, start=False, stop=False)
                last.then_inc(e_mm, 1)

            def down_pair(i):
                for u in range(2):
                    wait(pe, res_ok[u], i)
                    for c in range(CPB):
                        m = CPB * u + c
                        if isinstance(i, int) and m == 0:
                            first_chunk()
                            continue
                        pe.wait_ge(e_split, 6 * i + m + 1)
                        for t in range(ST):
                            for o in range(NB):
                                kt = c * NB + o
                                sl, at = 2 * NSL + kt // 3, (kt % 3) * H
                                hi, lo = w_hi[:, sl, at:at + H], w_lo[:, sl, at:at + H]
                                ts = slice(o * S + t * P, o * S + (t + 1) * P)
                                ah, al = o_hi[m % 2][:, ts], o_lo[m % 2][:, ts]
                                first, end = (c == 0 and o == 0), (c == CPB - 1 and o == NB - 1)
                                T.matmul(half[u][:, t, :], ah, hi, start=first, stop=False)
                                T.matmul(half[u][:, t, :], ah, lo, start=False, stop=False)
                                last = T.matmul(half[u][:, t, :], al, hi, start=False, stop=end)
                            if c == CPB - 1 and t < ST - 1:
                                last.then_inc(e_tile, 1)
                        last.then_inc(e_mm, 1)

            down_pair(0)
            with pe.Fori(1, B // 2) as i:
                down_pair(i)


def kernel(x, itok_B_0_6, L0_cond_down_w, L0_cond_down_b, L0_cond_up_w, L0_cond_up_b, L0_cond_ln_g,
           L0_cond_ln_b, L0_ffn_w_gate, L0_ffn_w_up, L0_ffn_w_down):
    import numpy as np
    import concourse.bacc as bacc
    from concourse.bass_utils import run_bass_kernel_spmd

    profiles = L0_cond_down_w.shape[0]

    def per_partition(v):
        return np.transpose(np.reshape(v, (profiles, HK, P)), (0, 2, 1))

    cols = np.concatenate([per_partition(L0_cond_ln_g), per_partition(L0_cond_ln_b),
                           np.reshape(L0_cond_down_b, (profiles, P, 1))], axis=2)

    def blocks_in(w):
        return np.reshape(np.transpose(np.reshape(w, (I, H // BLK, BLK)), (1, 0, 2)), (P, NS * BLK))

    def blocks_down(w):
        v = np.reshape(w, (H, NSL, 3, 4, BLK))
        return np.reshape(np.transpose(v, (1, 3, 2, 0, 4)), (P, NS * BLK))

    def slices_in(w):
        return np.reshape(np.transpose(w, (1, 0)), (NSL, P, SL))

    def slices_down(w):
        v = np.reshape(np.transpose(w, (1, 0)), (NSL, 3, P, H))
        return np.reshape(np.transpose(v, (0, 2, 1, 3)), (NSL, P, SL))

    arrays = {
        "x_in": x,
        "xT_in": np.transpose(x, (0, 2, 1)),
        "ids_in": np.reshape(itok_B_0_6, (1, B)),
        "down_w": L0_cond_down_w,
        "up_w": L0_cond_up_w,
        "up_b": L0_cond_up_b,
        "cols": cols,
        "w_blocks": np.stack([blocks_in(L0_ffn_w_gate), blocks_in(L0_ffn_w_up), blocks_down(L0_ffn_w_down)]),
        "w_slices": np.concatenate([slices_in(L0_ffn_w_gate), slices_in(L0_ffn_w_up), slices_down(L0_ffn_w_down)]),
    }
    arrays = {n: np.ascontiguousarray(a) for n, a in arrays.items()}
    nc = bacc.Bacc("TRN2", target_bir_lowering=False, num_devices=1)
    aps = [nc.dram_tensor(n, a.shape, mybir.dt.from_np(a.dtype), kind="ExternalInput").ap() for n, a in arrays.items()]
    out = nc.dram_tensor("out", (B, S, H), F32, kind="ExternalOutput").ap()
    adaln_ffn(nc, *aps, out)
    r = run_bass_kernel_spmd(nc, [arrays], core_ids=[0])
    return r.results[0]["out"]
```
